# Optimizing a Trainium2 kernel written in Bass

```python
import numpy as np
import jax
import jax.numpy as jnp

def _softmax(x, axis=-1):
    return jax.nn.softmax(x, axis=axis)

def _gelu(x):
    return jax.nn.gelu(x, approximate=True)

def _silu(x):
    return jax.nn.silu(x)

def _sigmoid(x):
    return jax.nn.sigmoid(x)

def _layernorm(x, axis=-1, eps=1e-05):
    m = jnp.mean(x, axis=axis, keepdims=True)
    v = jnp.var(x, axis=axis, keepdims=True)
    return (x - m) / jnp.sqrt(v + eps)

def _scatter_add(tgt, idx, src, axis=0):
    return tgt.at[idx].add(src)

def _segment_sum(src, seg, n):
    return jax.ops.segment_sum(src, seg, n)
kernel_name = 'mk_gnn_resnorm_d1_gnn_r32_0fced4'

def setup_inputs(seed: int=0):
    np.random.seed(seed)
    _w = jnp.asarray

    def _rec_inputs():
        import jax
        import jax.numpy as jnp
        _gk = jax.random.key(seed)
        x = -6.415e-05 + 1 * jax.random.normal(jax.random.fold_in(_gk, 1), (625, 512), jnp.float32)
        _s = jax.random.randint(jax.random.fold_in(_gk, 2), (10000,), 0, 625, jnp.int32)
        _d = jax.random.randint(jax.random.fold_in(_gk, 3), (10000,), 0, 625, jnp.int32)
        _loop = jnp.arange(625, dtype=jnp.int32)
        src = jnp.concatenate([_s, _d, _loop])
        dst = jnp.concatenate([_d, _s, _loop])
        _o = jnp.argsort(dst, stable=True)
        src = src[_o]
        dst = dst[_o]
        edge_type_8 = jax.random.randint(jax.random.fold_in(_gk, 12), (20625,), 0, 8, jnp.int32)
        return (x, src, dst, edge_type_8)
    x, src, dst, edge_type_8 = _rec_inputs()

    def _L0_gnn_setup():
        import jax, jax.numpy as jnp
        import numpy as np
        N = 625
        E = 5000
        D = 512
        R = 8
        key = jax.random.key(seed)
        ks = jax.random.split(key, 8)
        inp = {'input': jax.random.normal(ks[0], (N, D), dtype=jnp.float32), 'heads': jax.random.randint(ks[1], (E,), 0, N), 'tails': jax.random.randint(ks[2], (E,), 0, N), 'rel': jax.random.randint(ks[3], (E,), 0, R), 'W_self': jax.random.normal(ks[4], (D, D), dtype=jnp.float32) * 0.03, 'b_self': jnp.zeros((D,), dtype=jnp.float32), 'W_rel': jax.random.normal(ks[5], (2 * R, D, D), dtype=jnp.float32) * 0.03, 'b_rel': jnp.zeros((2 * R, D), dtype=jnp.float32)}
        return inp
    _L0_gnn_all = _L0_gnn_setup()
    _L0_gnn_in = {k: v for k, v in _L0_gnn_all.items() if k in ('W_self', 'b_self', 'W_rel', 'b_rel')}
    del _L0_gnn_all
    return {'x': x, 'src': src, 'dst': dst, 'edge_type_8': edge_type_8, 'L0_gnn_W_self': _L0_gnn_in['W_self'], 'L0_gnn_b_self': _L0_gnn_in['b_self'], 'L0_gnn_W_rel': _L0_gnn_in['W_rel'], 'L0_gnn_b_rel': _L0_gnn_in['b_rel']}

def reference(x, src, dst, edge_type_8, L0_gnn_W_self, L0_gnn_b_self, L0_gnn_W_rel, L0_gnn_b_rel):
    import jax
    import jax.numpy as jnp

    def _L0_gnn_ref(input, heads, tails, rel, W_self, b_self, W_rel, b_rel):
        import jax, jax.numpy as jnp
        import numpy as np
        N = 625
        E = 5000
        D = 512
        R = 8
        h_self = input @ W_self.T + b_self
        H_all = jnp.einsum('rod,nd->rno', W_rel, input) + b_rel[:, None, :]
        msg_to_heads = H_all[rel, tails]
        msg_to_tails = H_all[rel + R, heads]
        agg = jax.ops.segment_sum(msg_to_heads, heads, num_segments=N) + jax.ops.segment_sum(msg_to_tails, tails, num_segments=N)
        return jax.nn.relu(h_self + agg)
    x = _layernorm(x + _L0_gnn_ref(x, src, dst, edge_type_8, L0_gnn_W_self, L0_gnn_b_self, L0_gnn_W_rel, L0_gnn_b_rel), axis=-1)
    return x

_drawn_inputs = setup_inputs


def setup_inputs(seed=0):
    import zlib

    import numpy as np

    out = dict(_drawn_inputs(seed))
    spreads = {'L0_gnn_b_self': (0.0, 0.379), 'L0_gnn_b_rel': (0.0, 0.1)}
    factors = {}
    for name, (base, spread) in spreads.items():
        noise = np.random.default_rng([zlib.crc32(name.encode()), seed]).standard_normal(out[name].shape)
        drawn = base * np.exp(spread * noise) if base else spread * noise
        out[name] = jnp.asarray(drawn.astype(out[name].dtype))
    for name, factor in factors.items():
        out[name] = (out[name] * factor).astype(out[name].dtype)
    return out
```

```python
import concourse.bass as bass
from concourse import mybir
from contextlib import ExitStack

N = 625
D = 512
R = 8
E = 20625
P = 128
NB = (N + P - 1) // P
NP = NB * P
KD = D // P
LASTP = N - (NB - 1) * P

EP = 125
ET = E // EP
CH_T = 11
CHUNKS = ET // CH_T
CH_E = CH_T * EP
CH_S = CH_E + CH_E % 2
CH_BUF = 5

TS = 3
TW = 210
HALVES = CAP_T = 2
CAP = CAP_T * P
BUCKETS = R * NB * TS
COLS = BUCKETS * HALVES
MAX_ROUNDS = (E + CAP - 1) // CAP

SINGLES = 2 * R
SLOTS = 10
G1 = 3
RB = 5
BATCHES = ET // RB
RING_B = 3
GPR = SINGLES * NB
UPR = R * NB

X_SCALE = 2.0
W_SCALE = 32.0
H_SCALE = X_SCALE * W_SCALE
EPS = 1e-5

P2 = [("a", s) if s < 10 else (("h", (s - 10) // 2) if s % 2 == 0 else ("a", 10 + (s - 11) // 2))
      for s in range(20)]
P1C = [s - 3 if 3 <= s < 18 else None for s in range(20)]
A_STEPS = [(kind, hb) for hb in range(NB) for kind in ("A01", "A2", "T")]


def build(nc, x, xt, src, dst, et, w_self, b_self, w, b, out):
    f32, f16, i32 = mybir.dt.float32, mybir.dt.float16, mybir.dt.int32
    ALU = mybir.AluOpType
    ACT = mybir.ActivationFunctionType
    AX = mybir.AxisListType
    ds = bass.ds

    key_row = nc.dram_tensor("key_row", (CHUNKS, EP, CH_T), f16, kind="Internal").ap()

    ctx = ExitStack()
    with ctx:
        def sb(name, shape, dt):
            return ctx.enter_context(nc.sbuf_tensor(name, shape, dt))

        def sem(name):
            return ctx.enter_context(nc.semaphore(name))

        Hb = sb("Hb", [P, SLOTS, NB, 2, D], f16)

        def slot_f32(s, parts=P):
            return Hb[0:parts, s, :, :, :].rearrange("p m h d -> p (m h d)").bitcast(f32)

        x_stage = slot_f32(6).rearrange("p (k n) -> p k n", k=KD)
        bself = slot_f32(7)[:, 0:D]
        xn = slot_f32(6).rearrange("p (m d) -> p m d", m=NB)
        relu_o = slot_f32(7).rearrange("p (m d) -> p m d", m=NB)
        y = slot_f32(8).rearrange("p (m d) -> p m d", m=NB)
        o = slot_f32(9).rearrange("p (m d) -> p m d", m=NB)
        rank_raw = Hb[0:BUCKETS, 8:10, :, :, :].rearrange("p s m h d -> p (s m h d)")
        kbuf = rank_raw[:, 0:CH_BUF * CH_S].rearrange("p (c e) -> p c e", c=CH_BUF)[:, :, 0:CH_E]
        scan = rank_raw[:, CH_BUF * CH_S:CH_BUF * CH_S + 2 * CH_E].bitcast(f32)

        AB = sb("AB", [P, 2, 2, NB * NP], f16)
        A = [AB[:, p, 0, :].rearrange("p (m n) -> p m n", m=NB) for p in range(2)]
        AT = [AB[:, p, 1, :].rearrange("p (m n) -> p m n", m=NB) for p in range(2)]
        AB_flat = AB[:, :, :, :].rearrange("p a b n -> p (a b n)")
        RT_W = P + 2 * COLS
        route = AB_flat[0:EP, 0:RING_B * RB * RT_W].rearrange("p (b t w) -> p b t w", b=RING_B, t=RB)

        XT = sb("XT", [P, KD, 2, NP], f16)
        wf = sb("wf", [P, 2, KD * D], f32)
        whl = sb("whl", [P, 2, 2, KD * D], f16)
        bias = sb("bias", [P, 2, D], f32)
        t = sb("t", [P, 2, D], f32)
        acc = sb("acc", [P, NB, D], f32)
        ohh = sb("ohh", [P, 2, TS * HALVES, P], f16)
        oht = sb("oht", [P, 2, TS * HALVES, TW], f16)
        edges = sb("edges", [P, 2, COLS], f32)

        si = sb("si", [EP, ET], i32)
        di = sb("di", [EP, ET], i32)
        ei = sb("ei", [EP, ET], i32)
        hb_f = sb("hb_f", [EP, ET], f32)
        ts_f = sb("ts_f", [EP, ET], f32)
        tmp_f = sb("tmp_f", [EP, ET], f32)
        head1 = sb("head1", [EP, ET], f32)
        tail1 = sb("tail1", [EP, ET], f32)
        key = sb("key", [EP, CHUNKS, CH_T], f16)
        half = sb("half", [EP, ET], f32)
        lo1 = sb("lo1", [EP, ET], f32)
        col = sb("col", [EP, ET], f32)

        iota0 = sb("iota0", [P, 256], f16)
        iota1 = sb("iota1", [P, 256], f16)
        bucket_id = sb("bucket_id", [P, 1], f32)
        thresholds = sb("thresholds", [1, MAX_ROUNDS], f32)
        ident = sb("ident", [P, P], f16)
        ident_f = sb("ident_f", [P, P], f32)
        ones = sb("ones", [P, 2], f16)
        zeros = sb("zeros", [P, P], f16)
        zero_f = sb("zero_f", [P, 1], f32)
        offset = sb("offset", [P, 1], f32)
        carry = sb("carry", [P, 1], f32)
        total = sb("total", [P, 1], f32)
        most = sb("most", [1, 1], f32)
        over = sb("over", [1, MAX_ROUNDS], f32)
        rounds_f = sb("rounds_f", [1, 1], f32)
        rounds_i = sb("rounds_i", [1, 1], i32)
        stats = sb("stats", [P, NB, 6], f32)
        mv = sb("mv", [P, NB, 2], f32)
        sd = sb("sd", [P, NB], f32)
        rstd = sb("rstd", [P, NB], f32)

        bank = [ctx.enter_context(nc.psum_tensor(f"bank{i}", [P, 512], f32)) for i in range(8)]
        b_total, b_rank, b_sorted = bank[5], bank[6], bank[7]
        b_h2, b_a = bank[5], bank[6]
        b_t = bank[7][:, 0:NP // 2].bitcast(f16).rearrange("p (m n) -> p m n", m=NB)

        edges_in = sem("edges_in")
        x_in = sem("x_in")
        self_in = sem("self_in")
        w_in = [sem("w_in0"), sem("w_in1")]
        key_out = sem("key_out")
        key_in = [sem(f"key_in{c}") for c in range(CH_BUF)]
        xn_in = sem("xn_in")
        out_done = sem("out_done")
        const_done = sem("const_done")
        const_step = sem("const_step")
        x_hi = sem("x_hi")
        x_lo = sem("x_lo")
        w_hi = sem("w_hi")
        w_lo = sem("w_lo")
        small = sem("small")
        key_done = sem("key_done")
        h_mm = sem("h_mm")
        h_t = sem("h_t")
        h_hi = sem("h_hi")
        h_lo = sem("h_lo")
        mask_done = sem("mask_done")
        scan_done = sem("scan_done")
        carry_done = sem("carry_done")
        m_done = sem("m_done")
        rank_mm = sem("rank_mm")
        total_done = sem("total_done")
        total_mm = sem("total_mm")
        round_step = sem("round_step")
        rounds_done = sem("rounds_done")
        rounds_read = sem("rounds_read")
        place_step = sem("place_step")
        route_oh = sem("route_oh")
        route_mm = sem("route_mm")
        sorted_done = sem("sorted_done")
        a_oh = sem("a_oh")
        a_mm = sem("a_mm")
        a_ev = sem("a_ev")
        t_mm = sem("t_mm")
        t_ev = sem("t_ev")
        out_mm = sem("out_mm")
        acc_ev = sem("acc_ev")
        relu_done = sem("relu_done")
        fin_step = sem("fin_step")
        sd_done = sem("sd_done")
        o_done = sem("o_done")

        gates = sem("gates")

        block = ctx.enter_context(nc.Block())

        def gate(e):
            e.sem_inc(gates, 1)

        def rounds_loop(e):
            reg = e.alloc_register("rounds")
            e.reg_mov(reg, 1)
            return reg

        def p2_pairs(k, par):
            return 2 * k + par, (4 * k + 2 * par) % SLOTS

        @block.sync
        def _(sp):
            sp.dma_start(si[:, :], src).then_inc(edges_in, 16)
            sp.dma_start(di[:, :], dst).then_inc(edges_in, 16)
            sp.dma_start(ei[:, :], et).then_inc(edges_in, 16)
            sp.dma_start(x_stage, xt).then_inc(x_in, 16)
            sp.dma_start(wf[:, 1, :], w_self).then_inc(self_in, 16)
            sp.dma_start(wf[:, 0, :], w[0, :, :]).then_inc(w_in[0], 16)
            sp.dma_start(bself, b_self.to_broadcast([P, D])).then_inc(self_in, 16)
            sp.dma_start(bias[:, 0, :], b[0:1, :].to_broadcast([P, D])).then_inc(w_in[0], 16)
            reg = rounds_loop(sp)

            def load_w(S, s, slot):
                sp.wait_ge(w_lo, S)
                sp.dma_start(wf[:, slot, :], w[ds(s, 1), :, :].rearrange("a p n -> (a p) n"))\
                    .then_inc(w_in[slot], 16)
                sp.wait_ge(h_t, NB * S)
                sp.dma_start(bias[:, slot, :], b[ds(s, 1), :].to_broadcast([P, D]))\
                    .then_inc(w_in[slot], 16)

            with sp.Fori(0, reg) as rnd:
                with sp.Fori(0, G1) as it:
                    load_w(rnd * SINGLES + it * 2 + 1, it * 2 + 1, 1)
                    sp.wait_ge(key_out, 16)
                    sp.wait_ge(out_done, rnd * (16 * NB) + 1)
                    for c in range(CH_BUF):
                        sp.wait_ge(rank_mm, rnd * CHUNKS + it * CH_BUF + c + 1)
                        sp.dma_start(kbuf[:, c, :],
                                     key_row[ds(it * CH_BUF + c, 1), :, :]
                                     .rearrange("c p t -> c (p t)").to_broadcast([BUCKETS, CH_E]))\
                            .then_inc(key_in[c], 16)
                    load_w(rnd * SINGLES + it * 2 + 2, it * 2 + 2, 0)
                with sp.Fori(G1, R - 1) as it:
                    load_w(rnd * SINGLES + it * 2 + 1, it * 2 + 1, 1)
                    load_w(rnd * SINGLES + it * 2 + 2, it * 2 + 2, 0)
                load_w(rnd * SINGLES + SINGLES - 1, SINGLES - 1, 1)
                load_w(rnd * SINGLES + SINGLES, 0, 0)
                sp.wait_ge(h_mm, rnd * GPR + GPR + NB)
                sp.dma_start(xn[:, 0:NB - 1, :],
                             x[0:(NB - 1) * P, :].rearrange("(m p) d -> p m d", p=P)).then_inc(xn_in, 16)
                sp.dma_start(xn[0:LASTP, NB - 1, :], x[(NB - 1) * P:N, :]).then_inc(xn_in, 16)
                for m in range(NB):
                    sp.wait_ge(o_done, rnd * NB + m + 1)
                    rows = P if m < NB - 1 else LASTP
                    sp.dma_start(out[m * P:m * P + rows, :], o[0:rows, m, :]).then_inc(out_done, 16)
                sp.wait_ge(rounds_done, rnd + 1)
                gate(sp)
                sp.reg_load(reg, rounds_i[0:1, 0:1])
                sp.sem_inc(rounds_read, 1)
                sp.wait_ge(out_done, rnd * (16 * NB) + 16 * NB + 1)
                gate(sp)

        @block.gpsimd
        def _(pool):
            pool.sem_inc(h_lo, 2)
            pool.sem_inc(out_done, 1)
            iota = nc.gpsimd.iota
            iota(iota0[:, :], [[1, 256]], base=0, channel_multiplier=0,
                 allow_small_or_imprecise_dtypes=True).then_inc(const_done, 1)
            iota(iota1[:, :], [[1, 256]], base=1, channel_multiplier=0,
                 allow_small_or_imprecise_dtypes=True).then_inc(const_done, 1)
            iota(bucket_id[:, :], [[1, 1]], base=0, channel_multiplier=1,
                 allow_small_or_imprecise_dtypes=True).then_inc(const_done, 1)
            iota(thresholds[:, :], [[CAP, MAX_ROUNDS]], base=0, channel_multiplier=0,
                 allow_small_or_imprecise_dtypes=True).then_inc(const_done, 1)
            pool.memset(ones[:, :], 1.0).then_inc(const_done, 1)
            pool.memset(zeros[:, :], 0.0).then_inc(const_done, 1)
            pool.memset(zero_f[:, :], 0.0).then_inc(const_done, 1)
            pool.memset(offset[:, :], 0.0).then_inc(const_done, 1)
            pool.memset(ident[:, :], 0.0).then_inc(const_step, 1)
            pool.memset(ident_f[:, :], 0.0).then_inc(const_step, 1)
            pool.wait_ge(const_step, 2)
            for m in (ident, ident_f):
                pool.affine_select(out=m[:, :], in_=m[:, :], compare_op=ALU.not_equal, fill=1.0, base=0,
                                   pattern=[[-1, P]], channel_multiplier=1).then_inc(const_done, 1)
            reg = rounds_loop(pool)

            def low(n, slot, gg, m):
                pool.wait_ge(h_hi, n + 1)
                nc.gpsimd.tensor_tensor(Hb[:, ds(slot, 1), m, 1, :].rearrange("p a d -> p (a d)"),
                                        t[:, gg % 2, :],
                                        Hb[:, ds(slot, 1), m, 0, :].rearrange("p a d -> p (a d)"),
                                        ALU.subtract).then_inc(h_lo, 1)

            with pool.Fori(0, reg) as rnd:
                with pool.Fori(0, SLOTS // 2) as g:
                    for gg in range(2 * NB):
                        low(rnd * GPR + g * (2 * NB) + gg, g * 2 + gg // NB, gg, gg % NB)
                with pool.Fori(0, R - SLOTS // 2) as g:
                    for gg in range(2 * NB):
                        low(rnd * GPR + g * (2 * NB) + SLOTS * NB + gg, g * 2 + gg // NB, gg, gg % NB)
                pool.wait_ge(rounds_done, rnd + 1)
                gate(pool)
                pool.reg_load(reg, rounds_i[0:1, 0:1])
                pool.sem_inc(rounds_read, 1)

        @block.scalar
        def _(act):
            act.sem_inc(a_ev, 1)

            def split_w(source, slot):
                nc.scalar.activation(whl[:, slot, 0, :], source, ACT.Copy, scale=W_SCALE).then_inc(w_hi, 1)

            act.wait_ge(x_in, 16)
            nc.scalar.activation(XT[:, :, 0, :], x_stage, ACT.Copy, scale=X_SCALE).then_inc(x_hi, 1)
            act.wait_ge(self_in, 32)
            split_w(wf[:, 1, :], 1)
            act.wait_ge(w_in[0], 32)
            split_w(wf[:, 0, :], 0)
            act.wait_ge(key_done, 1)
            act.dma_start(key_row.rearrange("c p t -> p c t"), key[:, :, :]).then_inc(key_out, 16)
            reg = rounds_loop(act)

            def next_w(S, m, slot):
                act.wait_ge(w_in[slot], m * 32 + 32)
                act.wait_ge(h_mm, NB * S)
                split_w(wf[:, slot, :], slot)

            def high(n, slot, gg, m):
                act.wait_ge(h_t, n + NB + 1)
                nc.scalar.activation(Hb[:, ds(slot, 1), m, 0, :].rearrange("p a d -> p (a d)"),
                                     t[:, gg % 2, :], ACT.Copy).then_inc(h_hi, 1)

            def w_turn(rnd, G, gg):
                if gg == 1:
                    next_w(rnd * SINGLES + G * 2 + 1, rnd * R + G, 1)
                if gg == NB + 1:
                    next_w(rnd * SINGLES + G * 2 + 2, rnd * R + G + 1, 0)

            def unit_step(U, kind, hb, par):
                if kind == "A01":
                    act.wait_ge(a_mm, U * 2 + 4)
                    nc.scalar.activation(A[par][:, hb, 0:2 * TW], b_a[:, 0:2 * TW], ACT.Copy)\
                        .then_inc(a_ev, 1)
                if kind == "A2":
                    act.wait_ge(a_mm, U * 2 + 5)
                    nc.scalar.activation(A[par][:, hb, 2 * TW:3 * TW], b_a[:, 0:TW], ACT.Copy)\
                        .then_inc(a_ev, 1)

            with act.Fori(0, reg) as rnd:
                with act.Fori(0, G1 + 1) as G:
                    for gg in range(2 * NB):
                        high(rnd * GPR + G * (2 * NB) + gg, G * 2 + gg // NB, gg, gg % NB)
                        w_turn(rnd, G, gg)
                G = G1 + 1
                for s in range(20):
                    if s % 2:
                        gg = s // 2
                        high(rnd * GPR + G * 2 * NB + gg, G * 2 + gg // NB, gg, gg % NB)
                        w_turn(rnd, G, gg)
                    if P1C[s] is not None:
                        kind, hb = A_STEPS[P1C[s]]
                        unit_step(rnd * UPR + hb, kind, hb, 0)

                def relation(i, k, par, with_h):
                    for what, j in P2:
                        if what == "a":
                            kind, hb = A_STEPS[j]
                            unit_step(rnd * UPR + (i + 1) * NB + hb, kind, hb, 1 - par)
                        elif with_h:
                            gg = par * NB + j
                            high(rnd * GPR + k * (2 * NB) + SLOTS * NB + gg, k * 2 + par, gg, j)
                            w_turn(rnd, k + SLOTS // 2, gg)

                with act.Fori(0, 3) as k:
                    relation(k * 2, k, 0, True)
                    relation(k * 2 + 1, k, 1, True)
                relation(R - 2, 3, 0, False)

                def relu(m):
                    act.wait_ge(acc_ev, rnd * NB + m + 2)
                    if m == 0:
                        act.wait_ge(xn_in, rnd * 32 + 32)
                    nc.scalar.activation(relu_o[:, m, :], acc[:, m, :], ACT.Relu, scale=1.0 / H_SCALE)\
                        .then_inc(relu_done, 1)

                def deviation(m):
                    rows = P if m < NB - 1 else LASTP
                    act.wait_ge(fin_step, rnd * (5 * NB) + m * 5 + 4)
                    nc.scalar.activation(sd[0:rows, m:m + 1], mv[0:rows, m, 1:2], ACT.Sqrt)\
                        .then_inc(sd_done, 1)

                for m in range(NB):
                    relu(m)
                    if m:
                        deviation(m - 1)
                deviation(NB - 1)
                act.wait_ge(rounds_done, rnd + 1)
                gate(act)
                act.reg_load(reg, rounds_i[0:1, 0:1])
                act.sem_inc(rounds_read, 1)

        @block.vector
        def _(dve):
            v = nc.vector
            dve.sem_inc(t_ev, 1)
            dve.sem_inc(acc_ev, 1)
            dve.sem_inc(rounds_read, 1)
            steps = [0]

            def step(ins):
                steps[0] += 1
                ins.then_inc(small, 1)
                dve.wait_ge(small, steps[0])

            dve.wait_ge(edges_in, 48)
            step(v.tensor_scalar(hb_f[:, :], si[:, :], float(P), None, ALU.is_ge))
            for i in range(2, NB):
                step(v.scalar_tensor_tensor(hb_f[:, :], si[:, :], float(P * i), hb_f[:, :], ALU.is_ge, ALU.add))
            step(v.tensor_scalar(ts_f[:, :], di[:, :], float(TW), None, ALU.is_ge))
            step(v.scalar_tensor_tensor(ts_f[:, :], di[:, :], float(2 * TW), ts_f[:, :], ALU.is_ge, ALU.add))
            step(v.scalar_tensor_tensor(tmp_f[:, :], ei[:, :], float(NB * TS), ts_f[:, :], ALU.mult, ALU.add))
            v.scalar_tensor_tensor(key[:, :, :].rearrange("p c t -> p (c t)"), hb_f[:, :], float(TS),
                                   tmp_f[:, :], ALU.mult, ALU.add).then_inc(key_done, 1)
            step(v.tensor_scalar(head1[:, :], si[:, :], 1.0, None, ALU.add))
            step(v.scalar_tensor_tensor(head1[:, :], hb_f[:, :], -float(P), head1[:, :], ALU.mult, ALU.add))
            step(v.tensor_scalar(tail1[:, :], di[:, :], 1.0, None, ALU.add))
            step(v.scalar_tensor_tensor(tail1[:, :], ts_f[:, :], -float(TW), tail1[:, :], ALU.mult, ALU.add))

            def split_w(n, source, slot):
                dve.wait_ge(w_hi, n)
                v.scalar_tensor_tensor(whl[:, slot, 1, :], source, W_SCALE, whl[:, slot, 0, :],
                                       ALU.mult, ALU.subtract).then_inc(w_lo, 1)

            dve.wait_ge(x_hi, 1)
            for k in range(KD):
                v.scalar_tensor_tensor(XT[:, k, 1, :], x_stage[:, k, :], X_SCALE, XT[:, k, 0, :],
                                       ALU.mult, ALU.subtract).then_inc(x_lo, 1)
            split_w(1, wf[:, 1, :], 1)
            split_w(2, wf[:, 0, :], 0)
            dve.wait_ge(self_in, 32)
            for m in range(NB):
                dve.wait_ge(h_mm, m + 1)
                v.scalar_tensor_tensor(acc[:, m, :], bself, H_SCALE, bank[m][:, :], ALU.mult, ALU.add)\
                    .then_inc(h_t, 1)
            dve.wait_ge(const_done, 10)
            dve.wait_ge(key_done, 1)
            reg = rounds_loop(dve)

            def evacuate(n, gg, source):
                dve.wait_ge(h_mm, n + NB + 1)
                dve.wait_ge(h_lo, n + 1)
                v.scalar_tensor_tensor(t[:, gg % 2, :], bias[:, gg // NB % 2, :], H_SCALE, source[:, :],
                                       ALU.mult, ALU.add).then_inc(h_t, 1)

            def w_turn(rnd, G, gg):
                if gg == 1:
                    split_w(rnd * SINGLES + G * 2 + 3, wf[:, 1, :], 1)
                if gg == NB + 1:
                    split_w(rnd * SINGLES + G * 2 + 4, wf[:, 0, :], 0)

            def one_hots(U, u_local, par):
                dve.wait_ge(a_mm, U * 2 + 1)
                for j in range(TS * HALVES):
                    c = u_local * (TS * HALVES) + j
                    v.tensor_scalar(ohh[:, par, j, :], iota1[:, 0:P], edges[:, 0, ds(c, 1)], None,
                                    ALU.is_equal)
                    last = v.tensor_scalar(oht[:, par, j, :], iota1[:, 0:TW], edges[:, 1, ds(c, 1)], None,
                                           ALU.is_equal)
                last.then_inc(a_oh, 1)

            def transposes_out(U, hb, par):
                dve.wait_ge(t_mm, U + 1)
                v.tensor_copy(AT[par][:, :, hb * P:(hb + 1) * P], b_t).then_inc(t_ev, 1)

            with dve.Fori(0, reg) as rnd:
                v.tensor_copy(carry[0:BUCKETS, :], offset[0:BUCKETS, :]).then_inc(carry_done, 1)
                with dve.Fori(0, G1) as it:
                    for c in range(CH_BUF):
                        C = rnd * CHUNKS + it * CH_BUF + c
                        dve.wait_ge(carry_done, rnd * (CHUNKS + 1) + it * CH_BUF + c + 1)
                        dve.wait_ge(key_in[c], rnd * (16 * G1) + it * 16 + 16)
                        v.tensor_scalar(kbuf[:, c, :], kbuf[:, c, :], bucket_id[0:BUCKETS, :], None,
                                        ALU.is_equal).then_inc(mask_done, 1)
                        dve.wait_ge(mask_done, C + 1)
                        v.tensor_tensor_scan(scan, kbuf[:, c, :],
                                             zero_f[0:BUCKETS, :].to_broadcast([BUCKETS, CH_E]),
                                             carry[0:BUCKETS, :], ALU.add, ALU.add).then_inc(scan_done, 1)
                        dve.wait_ge(scan_done, C + 1)
                        v.tensor_copy(carry[0:BUCKETS, :], scan[:, CH_E - 1:CH_E]).then_inc(carry_done, 1)
                        v.scalar_tensor_tensor(kbuf[:, c, :], scan, 0.0, kbuf[:, c, :], ALU.max, ALU.mult)\
                            .then_inc(m_done, 1)
                        for gg in (2 * c, 2 * c + 1):
                            evacuate(rnd * GPR + it * (2 * NB) + gg, gg, bank[gg % NB])
                            w_turn(rnd, it, gg)
                        dve.wait_ge(m_done, C + 1)

                dve.wait_ge(carry_done, rnd * (CHUNKS + 1) + CHUNKS + 1)
                v.tensor_tensor(total[0:BUCKETS, :], carry[0:BUCKETS, :], offset[0:BUCKETS, :], ALU.subtract)\
                    .then_inc(total_done, 1)
                dve.wait_ge(total_done, rnd + 1)
                v.tensor_scalar(offset[:, :], offset[:, :], -float(CAP), None, ALU.add).then_inc(round_step, 1)
                dve.wait_ge(rank_mm, rnd * CHUNKS + CHUNKS + CH_BUF)
                v.tensor_scalar(half[:, :], b_rank[0:EP, 0:ET], float(P + 1), None, ALU.is_ge)\
                    .then_inc(place_step, 1)
                dve.wait_ge(place_step, rnd * 3 + 1)
                v.scalar_tensor_tensor(lo1[:, :], half[:, :], -float(P), b_rank[0:EP, 0:ET], ALU.mult, ALU.add)\
                    .then_inc(place_step, 1)
                v.scalar_tensor_tensor(col[:, :], key[:, :, :].rearrange("p c t -> p (c t)"), float(HALVES),
                                       half[:, :], ALU.mult, ALU.add).then_inc(place_step, 1)
                dve.wait_ge(total_mm, rnd + 1)
                v.tensor_reduce(most[:, :], b_total[0:1, 0:BUCKETS], AX.X, ALU.max).then_inc(round_step, 1)
                dve.wait_ge(round_step, rnd * 4 + 2)
                v.tensor_scalar(over[:, :], thresholds[:, :], most[0:1, 0:1], None, ALU.is_lt)\
                    .then_inc(round_step, 1)
                dve.wait_ge(round_step, rnd * 4 + 3)
                v.tensor_reduce(rounds_f[:, :], over[:, :], AX.X, ALU.add).then_inc(round_step, 1)
                dve.wait_ge(round_step, rnd * 4 + 4)
                dve.wait_ge(rounds_read, rnd * 4 + 1)
                v.tensor_copy(rounds_i[:, :], rounds_f[:, :]).then_inc(rounds_done, 1)
                dve.wait_ge(place_step, rnd * 3 + 3)

                def batch(B):
                    dve.wait_ge(route_mm, rnd * BATCHES + B + 1)
                    for i in range(RB):
                        j = B * RB + i
                        oh = route[:, B % RING_B, i, :]
                        v.tensor_scalar(oh[:, 0:P], iota1[0:EP, 0:P], lo1[:, j:j + 1], None, ALU.is_equal)
                        v.tensor_scalar(oh[:, P:P + COLS], iota0[0:EP, 0:COLS], col[:, j:j + 1],
                                        head1[:, j:j + 1], ALU.is_equal, ALU.mult)
                        last = v.tensor_scalar(oh[:, P + COLS:RT_W], iota0[0:EP, 0:COLS], col[:, j:j + 1],
                                               tail1[:, j:j + 1], ALU.is_equal, ALU.mult)
                    last.then_inc(route_oh, 1)

                for gg in range(2 * NB):
                    for B in range(3 * gg, 3 * gg + 3):
                        batch(B)
                    evacuate(rnd * GPR + G1 * 2 * NB + gg, gg, bank[gg % NB])
                    w_turn(rnd, G1, gg)
                for B in range(6 * NB, BATCHES):
                    batch(B)

                dve.wait_ge(route_mm, rnd * BATCHES + BATCHES + RING_B)
                for p in range(2):
                    v.memset(A[p][:, :, TS * TW:NP], 0.0)
                v.tensor_copy(edges[:, :, :].rearrange("p a c -> p (a c)"), b_sorted[:, 0:2 * COLS])\
                    .then_inc(sorted_done, 1)
                dve.wait_ge(sorted_done, rnd + 1)
                G = G1 + 1
                U = rnd * UPR
                one_hots(U, 0, 0)
                one_hots(U + 1, 1, 1)
                for s in range(20):
                    if s % 2:
                        gg = s // 2
                        evacuate(rnd * GPR + G * 2 * NB + gg, gg, bank[gg % NB])
                        w_turn(rnd, G, gg)
                    if P1C[s] is not None:
                        kind, hb = A_STEPS[P1C[s]]
                        if kind == "T":
                            transposes_out(U + hb, hb, 0)
                        if kind == "A2" and hb + 2 < NB:
                            one_hots(U + hb + 2, hb + 2, hb % 2)

                def relation(i, k, par, with_h):
                    u = (i + 1) * NB
                    up = (1 + par) % 2
                    one_hots(rnd * UPR + u, u, up)
                    one_hots(rnd * UPR + u + 1, u + 1, 1 - up)
                    for what, j in P2:
                        if what == "a":
                            kind, hb = A_STEPS[j]
                            if kind == "T":
                                transposes_out(rnd * UPR + u + hb, hb, 1 - par)
                            if kind == "A2" and hb + 2 < NB:
                                one_hots(rnd * UPR + u + hb + 2, u + hb + 2, (up + hb) % 2)
                        elif with_h:
                            gg = par * NB + j
                            evacuate(rnd * GPR + k * (2 * NB) + SLOTS * NB + gg, gg, b_h2)
                            w_turn(rnd, k + SLOTS // 2, gg)

                with dve.Fori(0, 3) as k:
                    relation(k * 2, k, 0, True)
                    relation(k * 2 + 1, k, 1, True)
                relation(R - 2, 3, 0, False)

                def messages(m):
                    dve.wait_ge(out_mm, rnd * NB + m + 1)
                    v.tensor_tensor(acc[:, m, :], acc[:, m, :], bank[m][:, :], ALU.add).then_inc(acc_ev, 1)

                def fin(m, n):
                    dve.wait_ge(fin_step, rnd * (5 * NB) + m * 5 + n)

                def statistics(m):
                    rows = P if m < NB - 1 else LASTP
                    dve.wait_ge(relu_done, rnd * NB + m + 1)
                    v.tensor_tensor(y[0:rows, m, :], relu_o[0:rows, m, :], xn[0:rows, m, :], ALU.add)\
                        .then_inc(fin_step, 1)
                    fin(m, 1)
                    v.bn_stats(stats[0:rows, m, :], y[0:rows, m, :]).then_inc(fin_step, 1)
                    fin(m, 2)
                    gate(dve)
                    v.bn_aggr(mv[0:rows, m, :], stats[0:rows, m, :]).then_inc(fin_step, 1)
                    fin(m, 3)
                    v.tensor_scalar(mv[0:rows, m, 1:2], mv[0:rows, m, 1:2], EPS, None, ALU.add)\
                        .then_inc(fin_step, 1)

                def normalise(m):
                    rows = P if m < NB - 1 else LASTP
                    dve.wait_ge(sd_done, rnd * NB + m + 1)
                    v.reciprocal(rstd[0:rows, m:m + 1], sd[0:rows, m:m + 1]).then_inc(fin_step, 1)
                    fin(m, 5)
                    v.tensor_scalar(o[0:rows, m, :], y[0:rows, m, :], mv[0:rows, m, 0:1],
                                    rstd[0:rows, m:m + 1], ALU.subtract, ALU.mult).then_inc(o_done, 1)

                for m in range(NB):
                    messages(m)
                    if m:
                        statistics(m - 1)
                        normalise(m - 1)
                statistics(NB - 1)
                normalise(NB - 1)
                dve.reg_load(reg, rounds_i[0:1, 0:1])
                dve.wait_ge(o_done, rnd * NB + NB)
                dve.wait_ge(round_step, rnd * 4 + 4)

        @block.tensor
        def _(pe):
            pe.sem_inc(rank_mm, CH_BUF)
            pe.sem_inc(route_mm, RING_B)
            pe.sem_inc(a_mm, 3)

            def h_products(dest, m, wslot, part=None):
                mm = []
                for k in range(KD):
                    for xh, wh in ((0, 0), (0, 1), (1, 0)):
                        mm.append((k, xh, wh))
                todo = mm if part is None else mm[part * 6:part * 6 + 6]
                for k, xh, wh in todo:
                    last = nc.tensor.matmul(dest[:, :], XT[:, k, xh, m * P:(m + 1) * P],
                                            whl[:, wslot, wh, k * D:(k + 1) * D],
                                            start=(k, xh, wh) == mm[0], stop=(k, xh, wh) == mm[-1])
                if part != 0:
                    last.then_inc(h_mm, 1)

            pe.wait_ge(x_lo, KD)
            pe.wait_ge(w_lo, 1)
            for m in range(NB):
                h_products(bank[m], m, 1)
            pe.wait_ge(const_done, 10)
            reg = rounds_loop(pe)

            def group(rnd, n, S, gg, part=None):
                if part != 1:
                    if gg % NB == 0:
                        pe.wait_ge(w_lo, S + 2)
                    pe.wait_ge(h_t, n + 1)
                h_products(bank[gg % NB], gg % NB, gg // NB, part)

            def unit_step(U, kind, hb, par, up):
                if kind == "A01":
                    pe.wait_ge(a_oh, U + 1)
                    pe.wait_ge(a_ev, U * 2 + 1)
                    for j in range(2 * HALVES):
                        ts = j // HALVES
                        last = nc.tensor.matmul(b_a[:, ts * TW:(ts + 1) * TW], ohh[:, up, j, :], oht[:, up, j, :],
                                                start=j % HALVES == 0, stop=j % HALVES == HALVES - 1)
                    last.then_inc(a_mm, 1)
                if kind == "A2":
                    pe.wait_ge(a_ev, U * 2 + 2)
                    for j in range(2 * HALVES, 3 * HALVES):
                        last = nc.tensor.matmul(b_a[:, 0:TW], ohh[:, up, j, :], oht[:, up, j, :],
                                                start=j % HALVES == 0, stop=j % HALVES == HALVES - 1)
                    last.then_inc(a_mm, 1)
                if kind == "T":
                    pe.wait_ge(a_ev, U * 2 + 3)
                    pe.wait_ge(t_ev, U + 1)
                    for tb in range(NB):
                        last = nc.tensor.transpose(b_t[:, tb, :], A[par][:, hb, tb * P:(tb + 1) * P], ident[:, :])
                    last.then_inc(t_mm, 1)

            with pe.Fori(0, reg) as rnd:
                pe.wait_ge(acc_ev, rnd * NB + 1)
                gate(pe)
                with pe.Fori(0, G1) as it:
                    for gg in range(2 * NB):
                        group(rnd, rnd * GPR + it * (2 * NB) + gg, rnd * SINGLES + it * 2 + gg // NB, gg)
                        if gg % 2:
                            c = gg // 2
                            pe.wait_ge(m_done, rnd * CHUNKS + it * CH_BUF + c + 1)
                            tiles = kbuf[:, c, :].rearrange("b (p t) -> b t p", t=CH_T)
                            for i in range(CH_T):
                                last = nc.tensor.matmul(b_rank[0:EP, ds(it * (CH_BUF * CH_T) + c * CH_T + i, 1)],
                                                        tiles[:, i, :], ones[0:BUCKETS, 0:1],
                                                        start=True, stop=True)
                            last.then_inc(rank_mm, 1)
                pe.wait_ge(total_done, rnd + 1)
                nc.tensor.matmul(b_total[0:1, 0:BUCKETS], total[0:BUCKETS, :], ident_f[0:BUCKETS, 0:BUCKETS],
                                 start=True, stop=True).then_inc(total_mm, 1)

                def batch(B):
                    pe.wait_ge(route_oh, rnd * BATCHES + B + 1)
                    for i in range(RB):
                        j = B * RB + i
                        oh = route[:, B % RING_B, i, :]
                        last = nc.tensor.matmul(b_sorted[:, 0:2 * COLS], oh[:, 0:P], oh[:, P:RT_W],
                                                start=j == 0, stop=j == ET - 1)
                    last.then_inc(route_mm, 1)

                for gg in range(2 * NB):
                    group(rnd, rnd * GPR + G1 * 2 * NB + gg, rnd * SINGLES + G1 * 2 + gg // NB, gg)
                    for B in range(3 * gg, 3 * gg + 3):
                        batch(B)
                for B in range(6 * NB, BATCHES):
                    batch(B)

                G = G1 + 1
                for s in range(20):
                    gg = s // 2
                    group(rnd, rnd * GPR + G * 2 * NB + gg, rnd * SINGLES + G * 2 + gg // NB, gg, s % 2)
                    if P1C[s] is not None:
                        kind, hb = A_STEPS[P1C[s]]
                        unit_step(rnd * UPR + hb, kind, hb, 0, hb % 2)

                pe.wait_ge(h_t, rnd * GPR + SLOTS * NB + NB)
                for m in range(NB):
                    nc.tensor.matmul(bank[m][:, :], zeros[:, :], whl[:, 0, 0, 0:D], start=True, stop=False,
                                     skip_group_check=True)

                def relation(i, k, slot, par, build_next, with_h):
                    up = (1 + par) % 2
                    pe.wait_ge(t_ev, rnd * UPR + (i + 1) * NB + 1)
                    pe.wait_ge(h_lo, rnd * GPR + (i * 2 + 1) * NB + 2)
                    for s, (what, j) in enumerate(P2):
                        if s == 10:
                            pe.wait_ge(h_lo, rnd * GPR + (i * 2 + 2) * NB + 2)
                        d, nb = s // 10, s % 10 // 2
                        lhs = (AT, A)[d][par]
                        for kb in ((0, 1, 2), (3, 4))[s % 2]:
                            for hl in range(2):
                                last = nc.tensor.matmul(
                                    bank[nb][:, :], lhs[:, kb, nb * P:(nb + 1) * P],
                                    Hb[:, ds(slot + d, 1), kb, hl, :].rearrange("p a d -> p (a d)"),
                                    start=False, stop=not build_next and s == 10 + nb * 2 + 1,
                                    skip_group_check=True)
                        if not build_next and s >= 10 and s % 2:
                            last.then_inc(out_mm, 1)
                        if what == "a" and build_next:
                            kind, hb = A_STEPS[j]
                            unit_step(rnd * UPR + (i + 1) * NB + hb, kind, hb, 1 - par, (up + hb) % 2)
                        if what == "h" and with_h:
                            if j == 0:
                                pe.wait_ge(w_lo, rnd * SINGLES + k * 2 + (SLOTS + par + 2))
                            pe.wait_ge(h_t, rnd * GPR + k * (2 * NB) + (SLOTS * NB + par * NB + j + NB))
                            h_products(b_h2, j, par)

                with pe.Fori(0, 3) as k:
                    relation(k * 2, k, k * 4, 0, True, True)
                    relation(k * 2 + 1, k, (k * 4 + 2) % SLOTS, 1, True, True)
                relation(R - 2, 3, 2, 0, True, False)
                relation(R - 1, 3, 4, 1, False, False)
                pe.wait_ge(rounds_done, rnd + 1)
                gate(pe)
                pe.reg_load(reg, rounds_i[0:1, 0:1])
                pe.sem_inc(rounds_read, 1)


def kernel(**inputs):
    import numpy as np
    import concourse.bacc as bacc
    from concourse import mybir
    from concourse.bass_utils import run_bass_kernel_spmd

    def tiles(a):
        return np.ascontiguousarray(np.asarray(a).reshape(EP, ET))

    def weights(a):
        a = np.asarray(a)
        a = np.swapaxes(a, -1, -2).reshape(*a.shape[:-2], KD, P, D)
        return np.ascontiguousarray(np.swapaxes(a, -2, -3).reshape(*a.shape[:-3], P, KD * D))

    order = [d * R + r for r in range(R) for d in range(2)]
    x = np.ascontiguousarray(inputs["x"])
    xt = np.zeros((KD, P, NP), x.dtype)
    xt[:, :, :N] = x.T.reshape(KD, P, N)
    arrays = {
        "x": x,
        "xt": np.ascontiguousarray(xt.transpose(1, 0, 2)),
        "src": tiles(inputs["src"]),
        "dst": tiles(inputs["dst"]),
        "et": tiles(inputs["edge_type_8"]),
        "w_self": weights(inputs["L0_gnn_W_self"]),
        "b_self": np.asarray(inputs["L0_gnn_b_self"]).reshape(1, D),
        "w": weights(inputs["L0_gnn_W_rel"])[order],
        "b": np.asarray(inputs["L0_gnn_b_rel"])[order],
    }
    arrays = {f"in_{k}_dram": np.ascontiguousarray(v) for k, v in arrays.items()}
    nc = bacc.Bacc("TRN2", target_bir_lowering=False, num_devices=1)
    args = [nc.dram_tensor(k, v.shape, mybir.dt.from_np(v.dtype), kind="ExternalInput").ap()
            for k, v in arrays.items()]
    out = nc.dram_tensor("out_dram", (N, D), mybir.dt.float32, kind="ExternalOutput").ap()
    build(nc, *args, out)
    result = run_bass_kernel_spmd(nc, [arrays], core_ids=[0])
    return result.results[0]["out_dram"]
```

```python
import concourse.bass as bass
from concourse import mybir
from contextlib import ExitStack

N = 625
D = 512
R = 8
E = 20625
P = 128
NB = (N + P - 1) // P
NP = NB * P
KD = D // P
LASTP = N - (NB - 1) * P

EP = 125
ET = E // EP
CH_T = 11
CHUNKS = 16
CH_E = CH_T * EP
CH_S = CH_E + CH_E % 2
CH_BUF = 8
CH_LAG = 2
SCANS = 4
NO_BUCKET = 200.0

TS = 3
TW = 210
HALVES = CAP_T = 2
CAP = CAP_T * P
BUCKETS = R * NB * TS
COLS = BUCKETS * HALVES
MAX_ROUNDS = (E + CAP - 1) // CAP

SINGLES = 2 * R
SLOTS = 10
G1 = 2
G2 = 4
RB = 3
BPP = 28
BATCHES = (G2 - G1) * BPP
ET_R = BATCHES * RB
RING_B = 7
B_MADE = [3, 3, 3, 3, 3, 3, 3, 3, 4, 0]
B_USED = [0, 3, 3, 3, 3, 3, 3, 3, 3, 4]
assert sum(B_MADE) == sum(B_USED) == BPP and G1 * CH_BUF == CHUNKS and CH_BUF + CH_LAG == 2 * NB
GPR = SINGLES * NB
UPR = R * NB

X_SCALE = 2.0
W_SCALE = 32.0
H_SCALE = X_SCALE * W_SCALE
EPS = 1e-5

P2 = [("a", s) if s < 10 else (("h", (s - 10) // 2) if s % 2 == 0 else ("a", 10 + (s - 11) // 2))
      for s in range(20)]
P1C = [s - 3 if 3 <= s < 18 else None for s in range(20)]
A_STEPS = [(kind, hb) for hb in range(NB) for kind in ("A01", "A2", "T")]


def build(nc, x, xt, src, dst, et, w_self, b_self, w, b, out):
    f32, f16, i32 = mybir.dt.float32, mybir.dt.float16, mybir.dt.int32
    ALU = mybir.AluOpType
    ACT = mybir.ActivationFunctionType
    AX = mybir.AxisListType
    ds = bass.ds

    key_row = nc.dram_tensor("key_row", (CHUNKS, EP, CH_T), f16, kind="Internal").ap()

    ctx = ExitStack()
    with ctx:
        def sb(name, shape, dt):
            return ctx.enter_context(nc.sbuf_tensor(name, shape, dt))

        def sem(name):
            return ctx.enter_context(nc.semaphore(name))

        Hb = sb("Hb", [P, SLOTS, NB, 2, D], f16)

        def slot_f32(s, parts=P):
            return Hb[0:parts, s, :, :, :].rearrange("p m h d -> p (m h d)").bitcast(f32)

        x_stage = slot_f32(6).rearrange("p (k n) -> p k n", k=KD)
        bself = slot_f32(5)[:, 0:D]
        xn = slot_f32(6).rearrange("p (m d) -> p m d", m=NB)
        xs = slot_f32(7).rearrange("p (m d) -> p m d", m=NB)
        y = slot_f32(8).rearrange("p (m d) -> p m d", m=NB)
        o = slot_f32(9).rearrange("p (m d) -> p m d", m=NB)
        rank_raw = Hb[0:BUCKETS, 7:10, :, :, :].rearrange("p s m h d -> p (s m h d)")
        kbuf = rank_raw[:, 0:CH_BUF * CH_S].rearrange("p (c e) -> p c e", c=CH_BUF)[:, :, 0:CH_E]


        AB = sb("AB", [P, 2, 2, NB * NP], f16)
        A = [AB[:, p, 0, :].rearrange("p (m n) -> p m n", m=NB) for p in range(2)]
        AT = [AB[:, p, 1, :].rearrange("p (m n) -> p m n", m=NB) for p in range(2)]
        AB_flat = AB[:, :, :, :].rearrange("p a b n -> p (a b n)")
        scan = AB_flat[0:BUCKETS, 0:2 * SCANS * CH_S].bitcast(f32).rearrange("p (c e) -> p c e", c=SCANS)[:, :, 0:CH_E]
        RT_W = 2 * P + COLS
        route = AB_flat[0:EP, 0:RING_B * RB * RT_W].rearrange("p (b t w) -> p b t w", b=RING_B, t=RB)

        XT = sb("XT", [P, KD, 2, NP], f16)
        wf = sb("wf", [P, 2, KD * D], f32)
        whl = sb("whl", [P, 2, 2, KD * D], f16)
        bias = sb("bias", [P, 2, D], f32)
        t = sb("t", [P, 2, D], f32)
        acc = sb("acc", [P, NB, D], f32)
        oh = sb("oh", [P, 2 * TS * HALVES * (P + TW)], f16)
        ohh = oh[:, 0:2 * TS * HALVES * P].rearrange("p (u t w) -> p u t w", u=2, t=TS * HALVES)
        oht = oh[:, 2 * TS * HALVES * P:].rearrange("p (u t w) -> p u t w", u=2, t=TS * HALVES)
        place = oh[0:EP, 0:RING_B * RB * P].rearrange("p (b t w) -> p b t w", b=RING_B, t=RB)
        edges = sb("edges", [P, 2, COLS], f32)

        si = sb("si", [EP, ET], i32)
        di = sb("di", [EP, ET], i32)
        ei = sb("ei", [EP, ET], i32)
        hb_f = sb("hb_f", [EP, ET], f32)
        ts_f = sb("ts_f", [EP, ET], f32)
        tmp_f = sb("tmp_f", [EP, ET], f32)
        head1 = sb("head1", [EP, ET_R], f32)
        tail1 = sb("tail1", [EP, ET_R], f32)
        key = sb("key", [EP, CHUNKS, CH_T], f16)
        half = sb("half", [EP, ET_R], f32)
        lo1 = sb("lo1", [EP, ET_R], f32)
        col = sb("col", [EP, ET_R], f32)

        iota0 = sb("iota0", [P, 256], f16)
        iota1 = sb("iota1", [P, 256], f16)
        bucket_id = sb("bucket_id", [P, 1], f32)
        thresholds = sb("thresholds", [1, MAX_ROUNDS], f32)
        ident = sb("ident", [P, P], f16)
        ident_f = sb("ident_f", [P, P], f32)
        ones = sb("ones", [P, 2], f16)
        zeros = sb("zeros", [P, P], f16)
        zero_f = sb("zero_f", [P, 1], f32)
        offset = sb("offset", [P, 1], f32)
        total = sb("total", [P, 1], f32)
        most = sb("most", [1, 1], f32)
        over = sb("over", [1, MAX_ROUNDS], f32)
        rounds_f = sb("rounds_f", [1, 1], f32)
        rounds_i = sb("rounds_i", [1, 1], i32)
        stats = sb("stats", [P, NB, 6], f32)
        mv = sb("mv", [P, NB, 2], f32)
        sd = sb("sd", [P, NB], f32)
        rstd = sb("rstd", [P, NB], f32)

        bank = [ctx.enter_context(nc.psum_tensor(f"bank{i}", [P, 512], f32)) for i in range(8)]
        b_rank, b_total, b_heads, b_tails = bank[6], bank[6][:, ET_R:ET_R + BUCKETS], bank[7], bank[5]
        b_h2, b_a = bank[5], bank[6]
        b_t = bank[7][:, 0:NP // 2].bitcast(f16).rearrange("p (m n) -> p m n", m=NB)

        edges_in = sem("edges_in")
        x_in = [sem(f"x_in{k}") for k in range(KD)]
        bself_in = sem("bself_in")
        w_in = [sem("w_in0"), sem("w_in1")]
        b_in = [sem("b_in0"), sem("b_in1")]
        key_out = sem("key_out")
        key_in = [sem(f"key_in{c}") for c in range(CH_BUF)]
        xn_in = sem("xn_in")
        out_done = sem("out_done")
        const_done = sem("const_done")
        const_step = sem("const_step")
        x_hi = sem("x_hi")
        x_lo = sem("x_lo")
        w_hi = sem("w_hi")
        w_lo = sem("w_lo")
        small = sem("small")
        key_done = sem("key_done")
        h_mm = sem("h_mm")
        h_t = sem("h_t")
        h_hi = sem("h_hi")
        h_lo = sem("h_lo")
        mask_done = sem("mask_done")
        scan_done = sem("scan_done")
        m_done = sem("m_done")
        rank_mm = sem("rank_mm")
        total_done = sem("total_done")
        total_mm = sem("total_mm")
        round_step = sem("round_step")
        rounds_done = sem("rounds_done")
        rounds_read = sem("rounds_read")
        place_step = sem("place_step")
        route_oh = sem("route_oh")
        route_h = sem("route_h")
        route_t = sem("route_t")
        route_mm = sem("route_mm")
        sorted_done = sem("sorted_done")
        a_oh = sem("a_oh")
        a_mm = sem("a_mm")
        a_ev = sem("a_ev")
        t_mm = sem("t_mm")
        t_ev = sem("t_ev")
        out_mm = sem("out_mm")
        acc_ev = sem("acc_ev")
        xs_done = sem("xs_done")
        pads = sem("pads")
        fin_step = sem("fin_step")
        sd_done = sem("sd_done")
        sd_first = sem("sd_first")
        o_done = sem("o_done")

        gates = sem("gates")

        block = ctx.enter_context(nc.Block())

        def gate(e):
            e.sem_inc(gates, 1)

        def rounds_loop(e):
            reg = e.alloc_register("rounds")
            e.reg_mov(reg, 1)
            return reg

        @block.sync
        def _(sp):
            for k in range(KD):
                sp.dma_start(x_stage[:, k, :], xt[:, k, :]).then_inc(x_in[k], 16)
                sp.dma_start(wf[:, 1, k * D:(k + 1) * D], w_self[:, k * D:(k + 1) * D]).then_inc(x_in[k], 16)
            sp.dma_start(wf[:, 0, :], w[0, :, :]).then_inc(w_in[0], 16)
            sp.dma_start(bself, b_self.to_broadcast([P, D])).then_inc(bself_in, 16)
            reg = rounds_loop(sp)

            def load_w(S, s, slot):
                sp.wait_ge(w_lo, KD * S)
                sp.dma_start(wf[:, slot, :], w[ds(s, 1), :, :].rearrange("a p n -> (a p) n"))\
                    .then_inc(w_in[slot], 16)

            with sp.Fori(0, reg) as rnd:
                with sp.Fori(0, G1) as it:
                    sp.wait_ge(key_out, 16)
                    sp.wait_ge(out_done, rnd * (16 * NB) + 1)
                    for c in range(CH_BUF):
                        sp.wait_ge(rank_mm, rnd * CHUNKS + it * CH_BUF + c + 1)
                        sp.dma_start(kbuf[:, c, :],
                                     key_row[ds(it * CH_BUF + c, 1), :, :]
                                     .rearrange("c p t -> c (p t)").to_broadcast([BUCKETS, CH_E]))\
                            .then_inc(key_in[c], 16)
                        if c == CH_BUF // 2 - 1:
                            load_w(rnd * SINGLES + it * 2 + 1, it * 2 + 1, 1)
                    load_w(rnd * SINGLES + it * 2 + 2, it * 2 + 2, 0)
                with sp.Fori(G1, R - 1) as it:
                    load_w(rnd * SINGLES + it * 2 + 1, it * 2 + 1, 1)
                    load_w(rnd * SINGLES + it * 2 + 2, it * 2 + 2, 0)
                load_w(rnd * SINGLES + SINGLES - 1, SINGLES - 1, 1)
                load_w(rnd * SINGLES + SINGLES, 0, 0)
                sp.wait_ge(h_mm, rnd * GPR + GPR + NB)
                sp.dma_start(xn[:, 0:NB - 1, :],
                             x[0:(NB - 1) * P, :].rearrange("(m p) d -> p m d", p=P)).then_inc(xn_in, 16)
                sp.dma_start(xn[0:LASTP, NB - 1, :], x[(NB - 1) * P:N, :]).then_inc(xn_in, 16)
                for m in range(NB):
                    sp.wait_ge(o_done, rnd * NB + m + 1)
                    rows = P if m < NB - 1 else LASTP
                    sp.dma_start(out[m * P:m * P + rows, :], o[0:rows, m, :]).then_inc(out_done, 16)
                sp.wait_ge(rounds_done, rnd + 1)
                gate(sp)
                sp.reg_load(reg, rounds_i[0:1, 0:1])
                sp.sem_inc(rounds_read, 1)
                sp.wait_ge(out_done, rnd * (16 * NB) + 16 * NB + 1)
                gate(sp)

        @block.gpsimd
        def _(pool):
            pool.sem_inc(h_lo, 2)
            pool.sem_inc(m_done, SCANS)
            pool.memset(zero_f[:, :], 0.0).then_inc(const_step, 1)
            pool.memset(key[:, CHUNKS - 1, :], NO_BUCKET).then_inc(pads, 1)
            for a in (head1, tail1):
                pool.memset(a[:, ET:ET_R], 0.0).then_inc(pads, 1)
            pool.sem_inc(out_done, 1)
            iota = nc.gpsimd.iota
            iota(iota0[:, :], [[1, 256]], base=0, channel_multiplier=0,
                 allow_small_or_imprecise_dtypes=True).then_inc(const_done, 1)
            iota(iota1[:, :], [[1, 256]], base=1, channel_multiplier=0,
                 allow_small_or_imprecise_dtypes=True).then_inc(const_done, 1)
            iota(bucket_id[:, :], [[1, 1]], base=0, channel_multiplier=1,
                 allow_small_or_imprecise_dtypes=True).then_inc(const_done, 1)
            iota(thresholds[:, :], [[CAP, MAX_ROUNDS]], base=0, channel_multiplier=0,
                 allow_small_or_imprecise_dtypes=True).then_inc(const_done, 1)
            pool.memset(ones[:, :], 1.0).then_inc(const_done, 1)
            pool.memset(zeros[:, :], 0.0).then_inc(const_done, 1)
            pool.memset(offset[:, :], 0.0).then_inc(const_done, 1)
            pool.memset(ident[:, :], 0.0).then_inc(const_step, 1)
            pool.memset(ident_f[:, :], 0.0).then_inc(const_step, 1)
            pool.wait_ge(const_step, 3)
            for m in (ident, ident_f):
                pool.affine_select(out=m[:, :], in_=m[:, :], compare_op=ALU.not_equal, fill=1.0, base=0,
                                   pattern=[[-1, P]], channel_multiplier=1).then_inc(const_done, 1)
            reg = rounds_loop(pool)

            def low(n, slot, gg, m):
                pool.wait_ge(h_hi, n + 1)
                nc.gpsimd.tensor_tensor(Hb[:, ds(slot, 1), m, 1, :].rearrange("p a d -> p (a d)"),
                                        t[:, gg % 2, :],
                                        Hb[:, ds(slot, 1), m, 0, :].rearrange("p a d -> p (a d)"),
                                        ALU.subtract).then_inc(h_lo, 1)

            with pool.Fori(0, reg) as rnd:
                with pool.Fori(0, G1) as it:
                    for gg in range(2 * NB):
                        if gg < CH_BUF:
                            pool.wait_ge(scan_done, rnd * (CHUNKS + 1) + it * CH_BUF + (gg + 2))
                            nc.gpsimd.tensor_tensor(kbuf[:, gg, :], scan[:, gg % SCANS, :], kbuf[:, gg, :],
                                                    ALU.mult).then_inc(m_done, 1)
                        low(rnd * GPR + it * (2 * NB) + gg, it * 2 + gg // NB, gg, gg % NB)
                with pool.Fori(G1, G2) as it:
                    B = 0
                    for gg in range(2 * NB):
                        for _ in range(B_MADE[gg]):
                            pool.wait_ge(route_oh, rnd * BATCHES + it * BPP + (B + 1 - G1 * BPP))
                            j = it * (BPP * RB) + (B * RB - G1 * BPP * RB)
                            nc.gpsimd.tensor_tensor(
                                route[:, B % RING_B, :, P:2 * P], place[:, B % RING_B, :, :],
                                tail1[:, ds(j, RB)].unsqueeze(2).to_broadcast([EP, RB, P]), ALU.mult)\
                                .then_inc(route_t, 1)
                            B += 1
                        low(rnd * GPR + it * (2 * NB) + gg, it * 2 + gg // NB, gg, gg % NB)
                for gg in range(2 * NB):
                    low(rnd * GPR + G2 * 2 * NB + gg, G2 * 2 + gg // NB, gg, gg % NB)
                with pool.Fori(0, R - SLOTS // 2) as g:
                    for gg in range(2 * NB):
                        low(rnd * GPR + g * (2 * NB) + SLOTS * NB + gg, g * 2 + gg // NB, gg, gg % NB)
                pool.wait_ge(rounds_done, rnd + 1)
                gate(pool)
                pool.reg_load(reg, rounds_i[0:1, 0:1])
                pool.sem_inc(rounds_read, 1)

        @block.scalar
        def _(act):
            act.sem_inc(a_ev, 1)

            act.dma_start(si[:, :], src).then_inc(edges_in, 16)
            act.dma_start(di[:, :], dst).then_inc(edges_in, 16)
            act.dma_start(ei[:, :], et).then_inc(edges_in, 16)
            act.dma_start(bias[:, 0, :], b[0:1, :].to_broadcast([P, D])).then_inc(b_in[0], 16)
            act.wait_ge(const_step, 1)
            nc.scalar.activation(sd[:, 0:1], zero_f[:, :], ACT.Sqrt).then_inc(sd_first, 1)

            def split_w(slot, k):
                nc.scalar.activation(whl[:, slot, 0, k * D:(k + 1) * D], wf[:, slot, k * D:(k + 1) * D],
                                     ACT.Copy, scale=W_SCALE).then_inc(w_hi, 1)

            for k in range(KD):
                act.wait_ge(x_in[k], 32)
                nc.scalar.activation(XT[:, k, 0, :], x_stage[:, k, :], ACT.Copy, scale=X_SCALE)\
                    .then_inc(x_hi, 1)
                nc.scalar.activation(whl[:, 1, 0, k * D:(k + 1) * D], wf[:, 1, k * D:(k + 1) * D], ACT.Copy,
                                     scale=W_SCALE).then_inc(x_hi, 1)
                if k == 1:
                    act.wait_ge(key_done, 1)
                    act.dma_start(key_row.rearrange("c p t -> p c t"), key[:, :, :]).then_inc(key_out, 16)
            act.wait_ge(w_in[0], 16)
            for k in range(KD):
                split_w(0, k)
            reg = rounds_loop(act)

            def next_w(S, s, m, slot, k):
                if k == 0:
                    act.wait_ge(w_in[slot], m * 16 + 16)
                    act.wait_ge(h_mm, NB * S)
                split_w(slot, k)
                if k == KD - 1:
                    act.wait_ge(h_t, NB * S)
                    act.dma_start(bias[:, slot, :], b[ds(s, 1), :].to_broadcast([P, D]))\
                        .then_inc(b_in[slot], 16)

            def high(n, slot, gg, m):
                act.wait_ge(h_t, n + NB + 1)
                nc.scalar.activation(Hb[:, ds(slot, 1), m, 0, :].rearrange("p a d -> p (a d)"),
                                     t[:, gg % 2, :], ACT.Copy).then_inc(h_hi, 1)

            def w_turn(rnd, G, gg):
                if gg < KD:
                    next_w(rnd * SINGLES + G * 2 + 1, G * 2 + 1, rnd * R + G, 1, gg)
                if NB <= gg < NB + KD:
                    next_w(rnd * SINGLES + G * 2 + 2, (G * 2 + 2) % SINGLES, rnd * R + G + 1, 0, gg - NB)

            def unit_step(U, kind, hb, par):
                if kind == "A01":
                    act.wait_ge(a_mm, U * 2 + 4)
                    nc.scalar.activation(A[par][:, hb, 0:2 * TW], b_a[:, 0:2 * TW], ACT.Copy)\
                        .then_inc(a_ev, 1)
                if kind == "A2":
                    act.wait_ge(a_mm, U * 2 + 5)
                    nc.scalar.activation(A[par][:, hb, 2 * TW:3 * TW], b_a[:, 0:TW], ACT.Copy)\
                        .then_inc(a_ev, 1)

            with act.Fori(0, reg) as rnd:
                with act.Fori(0, G1) as G:
                    for gg in range(2 * NB):
                        w_turn(rnd, G, gg)
                        high(rnd * GPR + G * (2 * NB) + gg, G * 2 + gg // NB, gg, gg % NB)
                with act.Fori(G1, G2) as G:
                    B = 0
                    for gg in range(2 * NB):
                        w_turn(rnd, G, gg)
                        for _ in range(B_MADE[gg]):
                            act.wait_ge(route_oh, rnd * BATCHES + G * BPP + (B + 1 - G1 * BPP))
                            for i in range(RB):
                                j = G * (BPP * RB) + (B * RB + i - G1 * BPP * RB)
                                last = nc.scalar.activation(
                                    route[:, B % RING_B, i, 0:P], place[:, B % RING_B, i, :], ACT.Copy,
                                    scale=head1[:, ds(j, 1)])
                            last.then_inc(route_h, 1)
                            B += 1
                        high(rnd * GPR + G * (2 * NB) + gg, G * 2 + gg // NB, gg, gg % NB)
                G = G2
                for s in range(20):
                    if s % 2:
                        gg = s // 2
                        w_turn(rnd, G, gg)
                        high(rnd * GPR + G * 2 * NB + gg, G * 2 + gg // NB, gg, gg % NB)
                    if P1C[s] is not None:
                        kind, hb = A_STEPS[P1C[s]]
                        unit_step(rnd * UPR + hb, kind, hb, 0)

                def relation(i, k, par, with_h):
                    for what, j in P2:
                        if what == "a":
                            kind, hb = A_STEPS[j]
                            unit_step(rnd * UPR + (i + 1) * NB + hb, kind, hb, 1 - par)
                        elif with_h:
                            gg = par * NB + j
                            w_turn(rnd, k + SLOTS // 2, gg)
                            high(rnd * GPR + k * (2 * NB) + SLOTS * NB + gg, k * 2 + par, gg, j)

                with act.Fori(0, 3) as k:
                    relation(k * 2, k, 0, True)
                    relation(k * 2 + 1, k, 1, True)
                relation(R - 2, 3, 0, False)

                act.wait_ge(xn_in, rnd * 32 + 32)
                for m in range(NB):
                    rows = P if m < NB - 1 else LASTP
                    nc.scalar.activation(xs[0:rows, m, :], xn[0:rows, m, :], ACT.Copy, scale=H_SCALE)\
                        .then_inc(xs_done, 1)
                for m in range(NB):
                    rows = P if m < NB - 1 else LASTP
                    act.wait_ge(fin_step, rnd * (5 * NB) + m * 5 + 4)
                    nc.scalar.activation(sd[0:rows, m:m + 1], mv[0:rows, m, 1:2], ACT.Sqrt)\
                        .then_inc(sd_done, 1)
                act.wait_ge(b_in[0], rnd * (16 * R) + 16 * R + 16)
                act.wait_ge(rounds_done, rnd + 1)
                gate(act)
                act.reg_load(reg, rounds_i[0:1, 0:1])
                act.sem_inc(rounds_read, 1)

        @block.vector
        def _(dve):
            v = nc.vector
            dve.sem_inc(t_ev, 1)
            dve.sem_inc(acc_ev, 1)
            dve.sem_inc(rounds_read, 1)
            steps = [0]

            def step(ins):
                steps[0] += 1
                ins.then_inc(small, 1)
                dve.wait_ge(small, steps[0])

            def x_part(k):
                dve.wait_ge(x_hi, 2 * k + 2)
                v.scalar_tensor_tensor(XT[:, k, 1, :], x_stage[:, k, :], X_SCALE, XT[:, k, 0, :],
                                       ALU.mult, ALU.subtract)
                v.scalar_tensor_tensor(whl[:, 1, 1, k * D:(k + 1) * D], wf[:, 1, k * D:(k + 1) * D], W_SCALE,
                                       whl[:, 1, 0, k * D:(k + 1) * D], ALU.mult, ALU.subtract)\
                    .then_inc(x_lo, 1)

            dve.wait_ge(edges_in, 48)
            dve.wait_ge(pads, 3)
            step(v.tensor_scalar(hb_f[:, :], si[:, :], float(P), None, ALU.is_ge))
            for i in range(2, NB):
                step(v.scalar_tensor_tensor(hb_f[:, :], si[:, :], float(P * i), hb_f[:, :], ALU.is_ge, ALU.add))
            x_part(0)
            step(v.tensor_scalar(ts_f[:, :], di[:, :], float(TW), None, ALU.is_ge))
            step(v.scalar_tensor_tensor(ts_f[:, :], di[:, :], float(2 * TW), ts_f[:, :], ALU.is_ge, ALU.add))
            step(v.scalar_tensor_tensor(tmp_f[:, :], ei[:, :], float(NB * TS), ts_f[:, :], ALU.mult, ALU.add))
            v.scalar_tensor_tensor(key[:, :, :].rearrange("p c t -> p (c t)")[:, 0:ET], hb_f[:, :], float(TS),
                                   tmp_f[:, :], ALU.mult, ALU.add).then_inc(key_done, 1)
            for k in range(1, KD):
                x_part(k)
            step(v.tensor_scalar(head1[:, 0:ET], si[:, :], 1.0, None, ALU.add))
            step(v.scalar_tensor_tensor(head1[:, 0:ET], hb_f[:, :], -float(P), head1[:, 0:ET], ALU.mult, ALU.add))
            step(v.tensor_scalar(tail1[:, 0:ET], di[:, :], 1.0, None, ALU.add))
            step(v.scalar_tensor_tensor(tail1[:, 0:ET], ts_f[:, :], -float(TW), tail1[:, 0:ET], ALU.mult, ALU.add))

            def split_w(n, slot, k):
                dve.wait_ge(w_hi, n * KD + (k + 1))
                v.scalar_tensor_tensor(whl[:, slot, 1, k * D:(k + 1) * D], wf[:, slot, k * D:(k + 1) * D],
                                       W_SCALE, whl[:, slot, 0, k * D:(k + 1) * D],
                                       ALU.mult, ALU.subtract).then_inc(w_lo, 1)

            dve.wait_ge(x_lo, KD)
            dve.sem_inc(w_lo, KD)
            for k in range(KD):
                split_w(0, 0, k)
            dve.wait_ge(bself_in, 16)
            for m in range(NB):
                dve.wait_ge(h_mm, m + 1)
                v.scalar_tensor_tensor(acc[:, m, :], bself, H_SCALE, bank[m][:, :], ALU.mult, ALU.add)\
                    .then_inc(h_t, 1)
            dve.wait_ge(const_done, 9)
            dve.wait_ge(key_done, 1)
            reg = rounds_loop(dve)

            def evacuate(rnd, G, gg, source, shift=0):
                n = rnd * GPR + G * (2 * NB) + (gg + shift)
                if gg % NB == 0:
                    m = rnd * R + G + shift // (2 * NB)
                    dve.wait_ge(b_in[gg // NB], m * 16 + 16)
                dve.wait_ge(h_mm, n + NB + 1)
                dve.wait_ge(h_lo, n + 1)
                v.scalar_tensor_tensor(t[:, gg % 2, :], bias[:, gg // NB % 2, :], H_SCALE, source[:, :],
                                       ALU.mult, ALU.add).then_inc(h_t, 1)

            def w_turn(rnd, G, gg):
                if gg < KD:
                    split_w(rnd * SINGLES + G * 2 + 1, 1, gg)
                if NB <= gg < NB + KD:
                    split_w(rnd * SINGLES + G * 2 + 2, 0, gg - NB)

            def mask_chunk(rnd, it, c):
                dve.wait_ge(key_in[c], rnd * (16 * G1) + it * 16 + 16)
                v.tensor_scalar(kbuf[:, c, :], kbuf[:, c, :], bucket_id[0:BUCKETS, :], None, ALU.is_equal)\
                    .then_inc(mask_done, 1)

            def count_chunk(rnd, it, c):
                C = rnd * CHUNKS + it * CH_BUF + c
                dve.wait_ge(mask_done, C + 1)
                dve.wait_ge(m_done, C + 1)
                dve.wait_ge(scan_done, C + rnd + 1)
                v.tensor_tensor_scan(scan[:, c % SCANS, :], kbuf[:, c, :],
                                     zero_f[0:BUCKETS, :].to_broadcast([BUCKETS, CH_E]),
                                     scan[:, (c - 1) % SCANS, CH_E - 1:CH_E], ALU.add, ALU.add)\
                    .then_inc(scan_done, 1)

            def one_hots(U, u_local, par):
                dve.wait_ge(a_mm, U * 2 + 1)
                T = TS * HALVES
                v.tensor_tensor(ohh[:, par, :, :], iota1[:, 0:P].unsqueeze(1).to_broadcast([P, T, P]),
                                edges[:, 0, ds(u_local * T, T)].unsqueeze(2).to_broadcast([P, T, P]),
                                ALU.is_equal)
                for j in range(T):
                    c = u_local * T + j
                    last = v.tensor_scalar(oht[:, par, j, :], iota1[:, 0:TW], edges[:, 1, ds(c, 1)], None,
                                           ALU.is_equal)
                last.then_inc(a_oh, 1)

            def transposes_out(U, hb, par):
                dve.wait_ge(t_mm, U + 1)
                v.tensor_copy(AT[par][:, :, hb * P:(hb + 1) * P], b_t).then_inc(t_ev, 1)

            with dve.Fori(0, reg) as rnd:
                v.tensor_copy(scan[:, SCANS - 1, CH_E - 1:CH_E], offset[0:BUCKETS, :]).then_inc(scan_done, 1)
                with dve.Fori(0, G1) as it:
                    mask_chunk(rnd, it, 0)
                    count_chunk(rnd, it, 0)
                    for gg in range(2 * NB):
                        evacuate(rnd, it, gg, bank[gg % NB])
                        if gg + 1 < CH_BUF:
                            mask_chunk(rnd, it, gg + 1)
                        w_turn(rnd, it, gg)
                        if gg + 1 < CH_BUF:
                            count_chunk(rnd, it, gg + 1)

                dve.wait_ge(scan_done, rnd * (CHUNKS + 1) + CHUNKS + 1)
                v.tensor_tensor(total[0:BUCKETS, :], scan[:, SCANS - 1, CH_E - 1:CH_E], offset[0:BUCKETS, :],
                                ALU.subtract).then_inc(total_done, 1)
                dve.wait_ge(total_done, rnd + 1)
                v.tensor_scalar(offset[:, :], offset[:, :], -float(CAP), None, ALU.add).then_inc(round_step, 1)
                dve.wait_ge(rank_mm, rnd * CHUNKS + CHUNKS + CH_BUF)
                v.tensor_scalar(half[:, :], b_rank[0:EP, 0:ET_R], float(P + 1), None, ALU.is_ge)\
                    .then_inc(place_step, 1)
                dve.wait_ge(place_step, rnd * 3 + 1)
                v.scalar_tensor_tensor(lo1[:, :], half[:, :], -float(P), b_rank[0:EP, 0:ET_R], ALU.mult, ALU.add)\
                    .then_inc(place_step, 1)
                v.scalar_tensor_tensor(col[:, :], key[:, :, :].rearrange("p c t -> p (c t)")[:, 0:ET_R], float(HALVES),
                                       half[:, :], ALU.mult, ALU.add).then_inc(place_step, 1)
                dve.wait_ge(place_step, rnd * 3 + 3)
                gate(dve)

                with dve.Fori(G1, G2) as it:
                    B = 0
                    for gg in range(2 * NB):
                        for _ in range(B_MADE[gg]):
                            dve.wait_ge(route_mm, rnd * BATCHES + it * BPP + (B + 1 - G1 * BPP))
                            j = it * (BPP * RB) + (B * RB - G1 * BPP * RB)
                            v.tensor_tensor(place[:, B % RING_B, :, :],
                                            iota1[0:EP, 0:P].unsqueeze(1).to_broadcast([EP, RB, P]),
                                            lo1[:, ds(j, RB)].unsqueeze(2).to_broadcast([EP, RB, P]),
                                            ALU.is_equal)
                            for i in range(RB):
                                last = v.tensor_scalar(route[:, B % RING_B, i, 2 * P:RT_W],
                                                       iota0[0:EP, 0:COLS], col[:, ds(j + i, 1)], None,
                                                       ALU.is_equal)
                            last.then_inc(route_oh, 1)
                            B += 1
                        w_turn(rnd, it, gg)
                        evacuate(rnd, it, gg, bank[gg % NB])

                dve.wait_ge(route_mm, rnd * BATCHES + BATCHES + RING_B)
                for p in range(2):
                    v.memset(A[p][:, :, TS * TW:NP], 0.0)
                v.tensor_copy(edges[:, 0, :], b_heads[:, 0:COLS]).then_inc(sorted_done, 1)
                v.tensor_copy(edges[:, 1, :], b_tails[:, 0:COLS]).then_inc(sorted_done, 1)
                dve.wait_ge(sorted_done, rnd * 2 + 2)
                G = G2
                U = rnd * UPR
                one_hots(U, 0, 0)
                one_hots(U + 1, 1, 1)
                dve.wait_ge(total_mm, rnd + 1)
                v.tensor_reduce(most[:, :], b_total[0:1, :], AX.X, ALU.max).then_inc(round_step, 1)
                dve.wait_ge(round_step, rnd * 4 + 2)
                v.tensor_scalar(over[:, :], thresholds[:, :], most[0:1, 0:1], None, ALU.is_lt)\
                    .then_inc(round_step, 1)
                dve.wait_ge(round_step, rnd * 4 + 3)
                v.tensor_reduce(rounds_f[:, :], over[:, :], AX.X, ALU.add).then_inc(round_step, 1)
                dve.wait_ge(round_step, rnd * 4 + 4)
                dve.wait_ge(rounds_read, rnd * 4 + 1)
                v.tensor_copy(rounds_i[:, :], rounds_f[:, :]).then_inc(rounds_done, 1)
                for s in range(20):
                    if s % 2:
                        gg = s // 2
                        evacuate(rnd, 0, gg, bank[gg % NB], G * 2 * NB)
                        w_turn(rnd, G, gg)
                    if P1C[s] is not None:
                        kind, hb = A_STEPS[P1C[s]]
                        if kind == "T":
                            transposes_out(U + hb, hb, 0)
                        if kind == "A2" and hb + 2 < NB:
                            one_hots(U + hb + 2, hb + 2, hb % 2)

                def relation(i, k, par, with_h):
                    u = (i + 1) * NB
                    up = (1 + par) % 2
                    one_hots(rnd * UPR + u, u, up)
                    one_hots(rnd * UPR + u + 1, u + 1, 1 - up)
                    for what, j in P2:
                        if what == "a":
                            kind, hb = A_STEPS[j]
                            if kind == "T":
                                transposes_out(rnd * UPR + u + hb, hb, 1 - par)
                            if kind == "A2" and hb + 2 < NB:
                                one_hots(rnd * UPR + u + hb + 2, u + hb + 2, (up + hb) % 2)
                        elif with_h:
                            gg = par * NB + j
                            evacuate(rnd, k, gg, b_h2, SLOTS * NB)
                            w_turn(rnd, k + SLOTS // 2, gg)

                with dve.Fori(0, 3) as k:
                    relation(k * 2, k, 0, True)
                    relation(k * 2 + 1, k, 1, True)
                relation(R - 2, 3, 0, False)

                def messages(m):
                    dve.wait_ge(out_mm, rnd * NB + m + 1)
                    v.tensor_tensor(acc[:, m, :], acc[:, m, :], bank[m][:, :], ALU.add).then_inc(acc_ev, 1)

                def fin(m, n):
                    dve.wait_ge(fin_step, rnd * (5 * NB) + m * 5 + n)

                def statistics(m):
                    rows = P if m < NB - 1 else LASTP
                    dve.wait_ge(xs_done, rnd * NB + m + 1)
                    dve.wait_ge(acc_ev, rnd * NB + m + 2)
                    v.scalar_tensor_tensor(y[0:rows, m, :], acc[0:rows, m, :], 0.0, xs[0:rows, m, :],
                                           ALU.max, ALU.add).then_inc(fin_step, 1)
                    fin(m, 1)
                    v.bn_stats(stats[0:rows, m, :], y[0:rows, m, :]).then_inc(fin_step, 1)
                    fin(m, 2)
                    gate(dve)
                    v.bn_aggr(mv[0:rows, m, :], stats[0:rows, m, :]).then_inc(fin_step, 1)
                    fin(m, 3)
                    v.tensor_scalar(mv[0:rows, m, 1:2], mv[0:rows, m, 1:2], EPS * H_SCALE ** 2, None, ALU.add)\
                        .then_inc(fin_step, 1)

                def normalise(m):
                    rows = P if m < NB - 1 else LASTP
                    dve.wait_ge(sd_first, 1)
                    dve.wait_ge(sd_done, rnd * NB + m + 1)
                    v.reciprocal(rstd[0:rows, m:m + 1], sd[0:rows, m:m + 1]).then_inc(fin_step, 1)
                    fin(m, 5)
                    v.tensor_scalar(o[0:rows, m, :], y[0:rows, m, :], mv[0:rows, m, 0:1],
                                    rstd[0:rows, m:m + 1], ALU.subtract, ALU.mult).then_inc(o_done, 1)

                for m in range(NB):
                    messages(m)
                    if m:
                        statistics(m - 1)
                        normalise(m - 1)
                statistics(NB - 1)
                normalise(NB - 1)
                dve.reg_load(reg, rounds_i[0:1, 0:1])
                dve.wait_ge(o_done, rnd * NB + NB)
                dve.wait_ge(round_step, rnd * 4 + 4)

        @block.tensor
        def _(pe):
            pe.sem_inc(rank_mm, CH_BUF)
            pe.sem_inc(route_mm, RING_B)
            pe.sem_inc(a_mm, 3)

            def h_products(dest, m, wslot, part=None):
                mm = []
                for k in range(KD):
                    for xh, wh in ((0, 0), (0, 1), (1, 0)):
                        mm.append((k, xh, wh))
                todo = mm if part is None else mm[part * 6:part * 6 + 6]
                for k, xh, wh in todo:
                    last = nc.tensor.matmul(dest[:, :], XT[:, k, xh, m * P:(m + 1) * P],
                                            whl[:, wslot, wh, k * D:(k + 1) * D],
                                            start=(k, xh, wh) == mm[0], stop=(k, xh, wh) == mm[-1])
                if part != 0:
                    last.then_inc(h_mm, 1)

            for k in range(KD):
                pe.wait_ge(x_lo, k + 1)
                for m in range(NB):
                    for xh, wh in ((0, 0), (0, 1), (1, 0)):
                        last = nc.tensor.matmul(bank[m][:, :], XT[:, k, xh, m * P:(m + 1) * P],
                                                whl[:, 1, wh, k * D:(k + 1) * D],
                                                start=(k, xh, wh) == (0, 0, 0), stop=(k, xh, wh) == (KD - 1, 1, 0))
                    if k == KD - 1:
                        last.then_inc(h_mm, 1)
            pe.wait_ge(const_done, 9)
            reg = rounds_loop(pe)

            def group(n, S, gg, part=None):
                if part != 1:
                    if gg % NB == 0:
                        pe.wait_ge(w_lo, S * KD + 2 * KD)
                    pe.wait_ge(h_t, n + 1)
                h_products(bank[gg % NB], gg % NB, gg // NB, part)

            def unit_step(U, kind, hb, par, up):
                if kind == "A01":
                    pe.wait_ge(a_oh, U + 1)
                    pe.wait_ge(a_ev, U * 2 + 1)
                    for j in range(2 * HALVES):
                        ts = j // HALVES
                        last = nc.tensor.matmul(b_a[:, ts * TW:(ts + 1) * TW], ohh[:, up, j, :], oht[:, up, j, :],
                                                start=j % HALVES == 0, stop=j % HALVES == HALVES - 1)
                    last.then_inc(a_mm, 1)
                if kind == "A2":
                    pe.wait_ge(a_ev, U * 2 + 2)
                    for j in range(2 * HALVES, 3 * HALVES):
                        last = nc.tensor.matmul(b_a[:, 0:TW], ohh[:, up, j, :], oht[:, up, j, :],
                                                start=j % HALVES == 0, stop=j % HALVES == HALVES - 1)
                    last.then_inc(a_mm, 1)
                if kind == "T":
                    pe.wait_ge(a_ev, U * 2 + 3)
                    pe.wait_ge(t_ev, U + 1)
                    for tb in range(NB):
                        last = nc.tensor.transpose(b_t[:, tb, :], A[par][:, hb, tb * P:(tb + 1) * P], ident[:, :])
                    last.then_inc(t_mm, 1)

            with pe.Fori(0, reg) as rnd:
                pe.wait_ge(acc_ev, rnd * NB + 1)
                gate(pe)
                with pe.Fori(0, G1) as it:
                    for gg in range(2 * NB):
                        group(rnd * GPR + it * (2 * NB) + gg, rnd * SINGLES + it * 2 + gg // NB, gg)
                        c = gg - CH_LAG
                        if c < 0:
                            continue
                        pe.wait_ge(m_done, rnd * CHUNKS + it * CH_BUF + (c + 1 + SCANS))
                        tiles = kbuf[:, c, :].rearrange("b (p t) -> b t p", t=CH_T)
                        for i in range(CH_T):
                            last = nc.tensor.matmul(b_rank[0:EP, ds(it * (CH_BUF * CH_T) + c * CH_T + i, 1)],
                                                    tiles[:, i, :], ones[0:BUCKETS, 0:1],
                                                    start=True, stop=True)
                        last.then_inc(rank_mm, 1)
                for dest in (b_heads, b_tails):
                    nc.tensor.matmul(dest[:, 0:COLS], zeros[:, :], whl[:, 0, 0, 0:COLS], start=True, stop=False,
                                     skip_group_check=True)


                with pe.Fori(G1, G2) as it:
                    B = 0
                    for gg in range(2 * NB):
                        group(rnd * GPR + it * (2 * NB) + gg, rnd * SINGLES + it * 2 + gg // NB, gg)
                        for _ in range(B_USED[gg]):
                            n = rnd * BATCHES + it * BPP + (B + 1 - G1 * BPP)
                            pe.wait_ge(route_h, n)
                            pe.wait_ge(route_t, n)
                            for i in range(RB):
                                o_h = route[:, B % RING_B, i, :]
                                nc.tensor.matmul(b_heads[:, 0:COLS], o_h[:, 0:P], o_h[:, 2 * P:RT_W],
                                                 start=False, stop=False, skip_group_check=True)
                                last = nc.tensor.matmul(b_tails[:, 0:COLS], o_h[:, P:2 * P], o_h[:, 2 * P:RT_W],
                                                        start=False, stop=False, skip_group_check=True)
                            last.then_inc(route_mm, 1)
                            B += 1

                pe.wait_ge(place_step, rnd * 3 + 2)
                pe.wait_ge(total_done, rnd + 1)
                nc.tensor.matmul(b_total[0:1, :], total[0:BUCKETS, :], ident_f[0:BUCKETS, 0:BUCKETS],
                                 start=True, stop=True).then_inc(total_mm, 1)

                G = G2
                for s in range(20):
                    if s == min(s for s in range(20) if P1C[s] is not None):
                        pe.wait_ge(round_step, rnd * 4 + 2)
                    gg = s // 2
                    group(rnd * GPR + G * 2 * NB + gg, rnd * SINGLES + G * 2 + gg // NB, gg, s % 2)
                    if P1C[s] is not None:
                        kind, hb = A_STEPS[P1C[s]]
                        unit_step(rnd * UPR + hb, kind, hb, 0, hb % 2)

                pe.wait_ge(h_t, rnd * GPR + SLOTS * NB + NB)
                for m in range(NB):
                    nc.tensor.matmul(bank[m][:, :], zeros[:, :], whl[:, 0, 0, 0:D], start=True, stop=False,
                                     skip_group_check=True)

                def relation(i, k, slot, par, build_next, with_h):
                    up = (1 + par) % 2
                    pe.wait_ge(t_ev, rnd * UPR + (i + 1) * NB + 1)
                    pe.wait_ge(h_lo, rnd * GPR + (i * 2 + 1) * NB + 2)
                    for s, (what, j) in enumerate(P2):
                        if s == 10:
                            pe.wait_ge(h_lo, rnd * GPR + (i * 2 + 2) * NB + 2)
                        d, nb = s // 10, s % 10 // 2
                        lhs = (AT, A)[d][par]
                        for kb in ((0, 1, 2), (3, 4))[s % 2]:
                            for hl in range(2):
                                last = nc.tensor.matmul(
                                    bank[nb][:, :], lhs[:, kb, nb * P:(nb + 1) * P],
                                    Hb[:, ds(slot + d, 1), kb, hl, :].rearrange("p a d -> p (a d)"),
                                    start=False, stop=not build_next and s == 10 + nb * 2 + 1,
                                    skip_group_check=True)
                        if not build_next and s >= 10 and s % 2:
                            last.then_inc(out_mm, 1)
                        if what == "a" and build_next:
                            kind, hb = A_STEPS[j]
                            unit_step(rnd * UPR + (i + 1) * NB + hb, kind, hb, 1 - par, (up + hb) % 2)
                        if what == "h" and with_h:
                            if j == 0:
                                pe.wait_ge(w_lo, rnd * (SINGLES * KD) + k * (2 * KD) + (SLOTS + par + 2) * KD)
                            pe.wait_ge(h_t, rnd * GPR + k * (2 * NB) + (SLOTS * NB + par * NB + j + NB))
                            h_products(b_h2, j, par)

                with pe.Fori(0, 3) as k:
                    relation(k * 2, k, k * 4, 0, True, True)
                    relation(k * 2 + 1, k, (k * 4 + 2) % SLOTS, 1, True, True)
                relation(R - 2, 3, 2, 0, True, False)
                relation(R - 1, 3, 4, 1, False, False)
                pe.wait_ge(rounds_done, rnd + 1)
                gate(pe)
                pe.reg_load(reg, rounds_i[0:1, 0:1])
                pe.sem_inc(rounds_read, 1)


def kernel(**inputs):
    import numpy as np
    import concourse.bacc as bacc
    from concourse import mybir
    from concourse.bass_utils import run_bass_kernel_spmd

    def tiles(a):
        return np.ascontiguousarray(np.asarray(a).reshape(EP, ET))

    def weights(a):
        a = np.asarray(a)
        a = np.swapaxes(a, -1, -2).reshape(*a.shape[:-2], KD, P, D)
        return np.ascontiguousarray(np.swapaxes(a, -2, -3).reshape(*a.shape[:-3], P, KD * D))

    order = [d * R + r for r in range(R) for d in range(2)]
    x = np.ascontiguousarray(inputs["x"])
    xt = np.zeros((KD, P, NP), x.dtype)
    xt[:, :, :N] = x.T.reshape(KD, P, N)
    arrays = {
        "x": x,
        "xt": np.ascontiguousarray(xt.transpose(1, 0, 2)),
        "src": tiles(inputs["src"]),
        "dst": tiles(inputs["dst"]),
        "et": tiles(inputs["edge_type_8"]),
        "w_self": weights(inputs["L0_gnn_W_self"]),
        "b_self": np.asarray(inputs["L0_gnn_b_self"]).reshape(1, D),
        "w": weights(inputs["L0_gnn_W_rel"])[order],
        "b": np.asarray(inputs["L0_gnn_b_rel"])[order],
    }
    arrays = {f"in_{k}_dram": np.ascontiguousarray(v) for k, v in arrays.items()}
    nc = bacc.Bacc("TRN2", target_bir_lowering=False, num_devices=1)
    args = [nc.dram_tensor(k, v.shape, mybir.dt.from_np(v.dtype), kind="ExternalInput").ap()
            for k, v in arrays.items()]
    out = nc.dram_tensor("out_dram", (N, D), mybir.dt.float32, kind="ExternalOutput").ap()
    build(nc, *args, out)
    result = run_bass_kernel_spmd(nc, [arrays], core_ids=[0])
    return result.results[0]["out_dram"]
```

```python
import concourse.bass as bass
from concourse import mybir
from contextlib import ExitStack

N = 625
D = 512
R = 8
E = 20625
P = 128
NB = (N + P - 1) // P
NP = NB * P
KD = D // P
LASTP = N - (NB - 1) * P

EP = 125
ET = E // EP
CH_T = 11
CHUNKS = 16
CH_E = CH_T * EP
CH_S = CH_E + CH_E % 2
CH_BUF = 8
CH_LAG = 2
SCANS = 4
SEED_LEAD = 3
SEEDS = 2 * NB - SEED_LEAD
WARM_UP = 40
NO_BUCKET = 200.0

TS = 3
TW = 210
HALVES = CAP_T = 2
CAP = CAP_T * P
BUCKETS = R * NB * TS
COLS = BUCKETS * HALVES
MAX_ROUNDS = (E + CAP - 1) // CAP

SINGLES = 2 * R
SLOTS = 10
G1 = 2
G2 = 4
RB = 3
BPP = 28
BATCHES = (G2 - G1) * BPP
ET_R = BATCHES * RB
RING_B = 7
B_MADE = [3, 3, 3, 3, 3, 3, 3, 3, 4, 0]
B_USED = [0, 3, 3, 3, 3, 3, 3, 3, 3, 4]
assert sum(B_MADE) == sum(B_USED) == BPP and G1 * CH_BUF == CHUNKS and CH_BUF + CH_LAG == 2 * NB
GPR = SINGLES * NB
UPR = R * NB

X_SCALE = 2.0
W_SCALE = 32.0
H_SCALE = X_SCALE * W_SCALE
EPS = 1e-5

P2 = [("a", s) if s < 10 else (("h", (s - 10) // 2) if s % 2 == 0 else ("a", 10 + (s - 11) // 2))
      for s in range(20)]
P1C = [s - 3 if 3 <= s < 18 else None for s in range(20)]
A_STEPS = [(kind, hb) for hb in range(NB) for kind in ("A01", "A2", "T")]


def build(nc, x, xt, src, dst, et, w_self, b_self, w, b, out):
    f32, f16, i32 = mybir.dt.float32, mybir.dt.float16, mybir.dt.int32
    ALU = mybir.AluOpType
    ACT = mybir.ActivationFunctionType
    AX = mybir.AxisListType
    ds = bass.ds

    key_row = nc.dram_tensor("key_row", (CHUNKS, EP, CH_T), f16, kind="Internal").ap()

    ctx = ExitStack()
    with ctx:
        def sb(name, shape, dt):
            return ctx.enter_context(nc.sbuf_tensor(name, shape, dt))

        def sem(name):
            return ctx.enter_context(nc.semaphore(name))

        Hb = sb("Hb", [P, SLOTS, NB, 2, D], f16)

        def slot_f32(s, parts=P):
            return Hb[0:parts, s, :, :, :].rearrange("p m h d -> p (m h d)").bitcast(f32)

        x_stage = slot_f32(6).rearrange("p (k n) -> p k n", k=KD)
        bself = slot_f32(5)[:, 0:D]
        xn = slot_f32(6).rearrange("p (m d) -> p m d", m=NB)
        xs = slot_f32(7).rearrange("p (m d) -> p m d", m=NB)
        y = slot_f32(8).rearrange("p (m d) -> p m d", m=NB)
        o = slot_f32(9).rearrange("p (m d) -> p m d", m=NB)
        rank_raw = Hb[0:BUCKETS, 7:10, :, :, :].rearrange("p s m h d -> p (s m h d)")
        kbuf = rank_raw[:, 0:CH_BUF * CH_S].rearrange("p (c e) -> p c e", c=CH_BUF)[:, :, 0:CH_E]


        AB = sb("AB", [P, 2, 2, NB * NP], f16)
        A = [AB[:, p, 0, :].rearrange("p (m n) -> p m n", m=NB) for p in range(2)]
        AT = [AB[:, p, 1, :].rearrange("p (m n) -> p m n", m=NB) for p in range(2)]
        AB_flat = AB[:, :, :, :].rearrange("p a b n -> p (a b n)")
        scan = AB_flat[0:BUCKETS, 0:2 * SCANS * CH_S].bitcast(f32).rearrange("p (c e) -> p c e", c=SCANS)[:, :, 0:CH_E]
        RT_W = 2 * P + COLS
        route = AB_flat[0:EP, 0:RING_B * RB * RT_W].rearrange("p (b t w) -> p b t w", b=RING_B, t=RB)

        XT = sb("XT", [P, KD, 2, NP], f16)
        wf = sb("wf", [P, 2, KD * D], f32)
        whl = sb("whl", [P, 2, 2, KD * D], f16)
        bias = sb("bias", [P, 2, D], f32)
        t = sb("t", [P, 2, D], f32)
        acc = sb("acc", [P, NB, D], f32)
        oh = sb("oh", [P, 2 * TS * HALVES * (P + TW)], f16)
        ohh = oh[:, 0:2 * TS * HALVES * P].rearrange("p (u t w) -> p u t w", u=2, t=TS * HALVES)
        oht = oh[:, 2 * TS * HALVES * P:].rearrange("p (u t w) -> p u t w", u=2, t=TS * HALVES)
        place = oh[0:EP, 0:RING_B * RB * P].rearrange("p (b t w) -> p b t w", b=RING_B, t=RB)
        edges = sb("edges", [P, 2, COLS], f32)

        si = sb("si", [EP, ET], i32)
        di = sb("di", [EP, ET], i32)
        ei = sb("ei", [EP, ET], i32)
        hb_f = sb("hb_f", [EP, ET], f32)
        ts_f = sb("ts_f", [EP, ET], f32)
        tmp_f = sb("tmp_f", [EP, ET], f32)
        head1 = sb("head1", [EP, ET_R], f32)
        tail1 = sb("tail1", [EP, ET_R], f32)
        key = sb("key", [EP, CHUNKS, CH_T], f16)
        half = sb("half", [EP, ET_R], f32)
        lo1 = sb("lo1", [EP, ET_R], f32)
        col = sb("col", [EP, ET_R], f32)

        iota0 = sb("iota0", [P, 256], f16)
        iota1 = sb("iota1", [P, 256], f16)
        bucket_id = sb("bucket_id", [P, 1], f32)
        thresholds = sb("thresholds", [1, MAX_ROUNDS], f32)
        ident = sb("ident", [P, P], f16)
        ident_f = sb("ident_f", [P, P], f32)
        ones = sb("ones", [P, 2], f16)
        zeros = sb("zeros", [P, P], f16)
        zero_f = sb("zero_f", [P, 1], f32)
        offset = sb("offset", [P, 1], f32)
        total = sb("total", [P, 1], f32)
        most = sb("most", [1, 1], f32)
        over = sb("over", [1, MAX_ROUNDS], f32)
        rounds_f = sb("rounds_f", [1, 1], f32)
        rounds_i = sb("rounds_i", [1, 1], i32)
        stats = sb("stats", [P, NB, 6], f32)
        mv = sb("mv", [P, NB, 2], f32)
        sd = sb("sd", [P, NB], f32)
        rstd = sb("rstd", [P, NB], f32)
        shift = sb("shift", [P, NB], f32)

        bank = [ctx.enter_context(nc.psum_tensor(f"bank{i}", [P, 512], f32)) for i in range(8)]
        b_rank, b_total, b_heads, b_tails = bank[6], bank[6][:, ET_R:ET_R + BUCKETS], bank[7], bank[5]
        b_h2, b_a = bank[5], bank[6]
        b_t = bank[7][:, 0:NP // 2].bitcast(f16).rearrange("p (m n) -> p m n", m=NB)

        src_in = sem("src_in")
        dst_in = sem("dst_in")
        x_in = [sem(f"x_in{k}") for k in range(KD)]
        ws_in = [sem(f"ws_in{k}") for k in range(KD)]
        bself_in = sem("bself_in")
        w_in = [sem("w_in0"), sem("w_in1")]
        b_in = [sem("b_in0"), sem("b_in1")]
        key_out = sem("key_out")
        key_in = [sem(f"key_in{c}") for c in range(CH_BUF)]
        xn_in = sem("xn_in")
        out_done = sem("out_done")
        const_done = sem("const_done")
        const_step = sem("const_step")
        zeros_done = sem("zeros_done")
        x_hi = sem("x_hi")
        x_lo = sem("x_lo")
        w_hi = sem("w_hi")
        w_lo = sem("w_lo")
        small = sem("small")
        key_done = sem("key_done")
        h_mm = sem("h_mm")
        h_seed = sem("h_seed")
        h_t = sem("h_t")
        h_hi = sem("h_hi")
        h_lo = sem("h_lo")
        mask_done = sem("mask_done")
        scan_done = sem("scan_done")
        m_done = sem("m_done")
        rank_mm = sem("rank_mm")
        total_done = sem("total_done")
        total_mm = sem("total_mm")
        round_step = sem("round_step")
        rounds_done = sem("rounds_done")
        rounds_read = sem("rounds_read")
        place_step = sem("place_step")
        route_oh = sem("route_oh")
        route_h = sem("route_h")
        route_t = sem("route_t")
        route_mm = sem("route_mm")
        sorted_done = sem("sorted_done")
        a_oh = sem("a_oh")
        a_mm = sem("a_mm")
        a_ev = sem("a_ev")
        t_mm = sem("t_mm")
        t_ev = sem("t_ev")
        out_mm = sem("out_mm")
        acc_in = sem("acc_in")
        acc_ev = sem("acc_ev")
        xs_done = sem("xs_done")
        pads = sem("pads")
        fin_step = sem("fin_step")
        sd_done = sem("sd_done")
        sd_first = sem("sd_first")
        o_done = sem("o_done")

        def fin_at(rnd, m, n):
            return rnd * (6 * NB - 1) + (m * 6 + n)

        gates = sem("gates")

        block = ctx.enter_context(nc.Block())

        def gate(e):
            e.sem_inc(gates, 1)

        def rounds_loop(e):
            reg = e.alloc_register("rounds")
            e.reg_mov(reg, 1)
            return reg

        @block.sync
        def _(sp):
            for k in range(KD):
                sp.dma_start(x_stage[:, k, :], xt[:, k, :]).then_inc(x_in[k], 16)
                sp.dma_start(wf[:, 1, k * D:(k + 1) * D], w_self[:, k * D:(k + 1) * D]).then_inc(ws_in[k], 16)
            sp.dma_start(wf[:, 0, :], w[0, :, :]).then_inc(w_in[0], 16)
            sp.dma_start(bself, b_self.to_broadcast([P, D])).then_inc(bself_in, 16)
            reg = rounds_loop(sp)

            def load_w(S, s, slot):
                sp.wait_ge(w_lo, KD * S)
                sp.dma_start(wf[:, slot, :], w[ds(s, 1), :, :].rearrange("a p n -> (a p) n"))\
                    .then_inc(w_in[slot], 16)

            with sp.Fori(0, reg) as rnd:
                with sp.Fori(0, G1) as it:
                    sp.wait_ge(key_out, 16)
                    sp.wait_ge(out_done, rnd * (16 * NB) + 1)
                    for c in range(CH_BUF):
                        sp.wait_ge(rank_mm, rnd * CHUNKS + it * CH_BUF + c + 1)
                        sp.dma_start(kbuf[:, c, :],
                                     key_row[ds(it * CH_BUF + c, 1), :, :]
                                     .rearrange("c p t -> c (p t)").to_broadcast([BUCKETS, CH_E]))\
                            .then_inc(key_in[c], 16)
                        if c == CH_BUF // 2 - 1:
                            load_w(rnd * SINGLES + it * 2 + 1, it * 2 + 1, 1)
                    load_w(rnd * SINGLES + it * 2 + 2, it * 2 + 2, 0)
                with sp.Fori(G1, R - 1) as it:
                    load_w(rnd * SINGLES + it * 2 + 1, it * 2 + 1, 1)
                    load_w(rnd * SINGLES + it * 2 + 2, it * 2 + 2, 0)
                load_w(rnd * SINGLES + SINGLES - 1, SINGLES - 1, 1)
                load_w(rnd * SINGLES + SINGLES, 0, 0)
                sp.wait_ge(h_mm, rnd * GPR + GPR + NB)
                sp.dma_start(xn[:, 0:NB - 1, :],
                             x[0:(NB - 1) * P, :].rearrange("(m p) d -> p m d", p=P)).then_inc(xn_in, 16)
                sp.dma_start(xn[0:LASTP, NB - 1, :], x[(NB - 1) * P:N, :]).then_inc(xn_in, 16)
                for m in range(NB):
                    sp.wait_ge(o_done, rnd * NB + m + 1)
                    rows = P if m < NB - 1 else LASTP
                    sp.dma_start(out[m * P:m * P + rows, :], o[0:rows, m, :]).then_inc(out_done, 16)
                sp.wait_ge(rounds_done, rnd + 1)
                gate(sp)
                sp.reg_load(reg, rounds_i[0:1, 0:1])
                sp.sem_inc(rounds_read, 1)
                sp.wait_ge(out_done, rnd * (16 * NB) + 16 * NB + 1)
                gate(sp)

        @block.gpsimd
        def _(pool):
            pool.sem_inc(h_lo, 2)
            pool.sem_inc(m_done, SCANS)
            pool.memset(zero_f[:, :], 0.0).then_inc(const_step, 1)
            pool.memset(key[:, CHUNKS - 1, :], NO_BUCKET).then_inc(pads, 1)
            for a in (head1, tail1):
                pool.memset(a[:, ET:ET_R], 0.0).then_inc(pads, 1)
            pool.sem_inc(out_done, 1)
            iota = nc.gpsimd.iota
            iota(iota0[:, :], [[1, 256]], base=0, channel_multiplier=0,
                 allow_small_or_imprecise_dtypes=True).then_inc(const_done, 1)
            iota(iota1[:, :], [[1, 256]], base=1, channel_multiplier=0,
                 allow_small_or_imprecise_dtypes=True).then_inc(const_done, 1)
            iota(bucket_id[:, :], [[1, 1]], base=0, channel_multiplier=1,
                 allow_small_or_imprecise_dtypes=True).then_inc(const_done, 1)
            iota(thresholds[:, :], [[CAP, MAX_ROUNDS]], base=0, channel_multiplier=0,
                 allow_small_or_imprecise_dtypes=True).then_inc(const_done, 1)
            pool.memset(ones[:, :], 1.0).then_inc(const_done, 1)
            pool.memset(offset[:, :], 0.0).then_inc(const_done, 1)
            pool.memset(ident[:, :], 0.0).then_inc(const_step, 1)
            pool.memset(ident_f[:, :], 0.0).then_inc(const_step, 1)
            pool.wait_ge(const_step, 3)
            for m in (ident, ident_f):
                pool.affine_select(out=m[:, :], in_=m[:, :], compare_op=ALU.not_equal, fill=1.0, base=0,
                                   pattern=[[-1, P]], channel_multiplier=1).then_inc(const_done, 1)
            reg = rounds_loop(pool)

            def low(n, slot, gg, m):
                pool.wait_ge(h_hi, n + 1)
                nc.gpsimd.tensor_tensor(Hb[:, ds(slot, 1), m, 1, :].rearrange("p a d -> p (a d)"),
                                        t[:, gg % 2, :],
                                        Hb[:, ds(slot, 1), m, 0, :].rearrange("p a d -> p (a d)"),
                                        ALU.subtract).then_inc(h_lo, 1)

            with pool.Fori(0, reg) as rnd:
                with pool.Fori(0, G1) as it:
                    for gg in range(CH_BUF):
                        pool.wait_ge(scan_done, rnd * (CHUNKS + 1) + it * CH_BUF + (gg + 2))
                        nc.gpsimd.tensor_tensor(kbuf[:, gg, :], scan[:, gg % SCANS, :], kbuf[:, gg, :],
                                                ALU.mult).then_inc(m_done, 1)
                        if gg == 1:
                            low(rnd * GPR + it * (2 * NB), it * 2, 0, 0)
                    for gg in range(1, SEED_LEAD):
                        low(rnd * GPR + it * (2 * NB) + gg, it * 2, gg, gg)
                    pool.wait_ge(h_t, rnd * GPR + it * (2 * NB) + 3 * NB)
                    pool.wait_ge(h_lo, rnd * GPR + it * (2 * NB) + (SEED_LEAD + 2))
                    pool.sem_inc(h_lo, SEEDS)
                with pool.Fori(G1, G2) as it:
                    B = 0
                    for gg in range(2 * NB):
                        for _ in range(B_MADE[gg]):
                            pool.wait_ge(route_oh, rnd * BATCHES + it * BPP + (B + 1 - G1 * BPP))
                            j = it * (BPP * RB) + (B * RB - G1 * BPP * RB)
                            nc.gpsimd.tensor_tensor(
                                route[:, B % RING_B, :, P:2 * P], place[:, B % RING_B, :, :],
                                tail1[:, ds(j, RB)].unsqueeze(2).to_broadcast([EP, RB, P]), ALU.mult)\
                                .then_inc(route_t, 1)
                            B += 1
                        low(rnd * GPR + it * (2 * NB) + gg, it * 2 + gg // NB, gg, gg % NB)
                for gg in range(2 * NB):
                    low(rnd * GPR + G2 * 2 * NB + gg, G2 * 2 + gg // NB, gg, gg % NB)
                with pool.Fori(0, R - SLOTS // 2) as g:
                    for gg in range(2 * NB):
                        low(rnd * GPR + g * (2 * NB) + SLOTS * NB + gg, g * 2 + gg // NB, gg, gg % NB)
                pool.wait_ge(rounds_done, rnd + 1)
                gate(pool)
                pool.reg_load(reg, rounds_i[0:1, 0:1])
                pool.sem_inc(rounds_read, 1)

        @block.scalar
        def _(act):
            act.sem_inc(a_ev, 1)
            act.sem_inc(acc_ev, 1)

            act.wait_ge(const_step, 1)
            nc.scalar.activation(sd[:, 0:1], zero_f[:, :], ACT.Sqrt).then_inc(sd_first, 1)
            act.dma_start(si[:, :], src).then_inc(src_in, 16)
            act.dma_start(di[:, :], dst).then_inc(dst_in, 16)
            act.dma_start(ei[:, :], et).then_inc(dst_in, 16)

            def split_w(slot, k):
                nc.scalar.activation(whl[:, slot, 0, k * D:(k + 1) * D], wf[:, slot, k * D:(k + 1) * D],
                                     ACT.Copy, scale=W_SCALE).then_inc(w_hi, 1)

            for k in range(KD):
                act.wait_ge(x_in[k], 16)
                nc.scalar.activation(XT[:, k, 0, :], x_stage[:, k, :], ACT.Copy, scale=X_SCALE)\
                    .then_inc(x_hi, 1)
                act.wait_ge(ws_in[k], 16)
                nc.scalar.activation(whl[:, 1, 0, k * D:(k + 1) * D], wf[:, 1, k * D:(k + 1) * D], ACT.Copy,
                                     scale=W_SCALE).then_inc(x_hi, 1)
                if k == 1:
                    act.wait_ge(key_done, 1)
                    act.dma_start(key_row.rearrange("c p t -> p c t"), key[:, :, :]).then_inc(key_out, 16)
                    act.dma_start(bias[:, 0, :], b[0:1, :].to_broadcast([P, D])).then_inc(b_in[0], 16)
            act.wait_ge(w_in[0], 16)
            for k in range(KD):
                split_w(0, k)
            reg = rounds_loop(act)

            def next_w(S, s, m, slot, k, bias_k=KD - 1):
                if k == 0:
                    act.wait_ge(w_in[slot], m * 16 + 16)
                    act.wait_ge(h_mm, NB * S)
                split_w(slot, k)
                if k == bias_k:
                    act.wait_ge(h_t, NB * S)
                    act.dma_start(bias[:, slot, :], b[ds(s, 1), :].to_broadcast([P, D]))\
                        .then_inc(b_in[slot], 16)

            def high(n, slot, gg, m):
                act.wait_ge(h_t, n + NB + 1)
                nc.scalar.activation(Hb[:, ds(slot, 1), m, 0, :].rearrange("p a d -> p (a d)"),
                                     t[:, gg % 2, :], ACT.Copy).then_inc(h_hi, 1)

            def w_turn(rnd, G, gg, bias_k=KD - 1):
                if gg < KD:
                    next_w(rnd * SINGLES + G * 2 + 1, G * 2 + 1, rnd * R + G, 1, gg, bias_k)
                if NB <= gg < NB + KD:
                    next_w(rnd * SINGLES + G * 2 + 2, (G * 2 + 2) % SINGLES, rnd * R + G + 1, 0, gg - NB)

            def unit_step(U, kind, hb, par):
                if kind == "A01":
                    act.wait_ge(a_mm, U * 2 + 4)
                    nc.scalar.activation(A[par][:, hb, 0:2 * TW], b_a[:, 0:2 * TW], ACT.Copy)\
                        .then_inc(a_ev, 1)
                if kind == "A2":
                    act.wait_ge(a_mm, U * 2 + 5)
                    nc.scalar.activation(A[par][:, hb, 2 * TW:3 * TW], b_a[:, 0:TW], ACT.Copy)\
                        .then_inc(a_ev, 1)

            with act.Fori(0, reg) as rnd:
                with act.Fori(0, G1) as G:
                    for gg in range(2 * NB):
                        n = rnd * GPR + G * (2 * NB) + gg
                        w_turn(rnd, G, gg, 0)
                        if gg < SEEDS:
                            to = gg + SEED_LEAD
                            if to % NB == 0 or gg == 0:
                                act.wait_ge(b_in[to // NB], (rnd * R + G) * 16 + 16)
                            act.wait_ge(h_t, n + (SEED_LEAD + 1))
                            nc.scalar.activation(bank[to % NB][:, :], bias[:, to // NB, :], ACT.Copy,
                                                 scale=H_SCALE).then_inc(h_seed, 1)
                        if gg < SEED_LEAD:
                            high(n, G * 2 + gg // NB, gg, gg % NB)
                        else:
                            act.wait_ge(h_mm, n + (NB + 1))
                            nc.scalar.activation(
                                Hb[:, ds(G * 2 + gg // NB, 1), gg % NB, 0, :].rearrange("p a d -> p (a d)"),
                                bank[gg % NB][:, :], ACT.Copy).then_inc(h_hi, 1)
                with act.Fori(G1, G2) as G:
                    B = 0
                    for gg in range(2 * NB):
                        w_turn(rnd, G, gg)
                        for _ in range(B_MADE[gg]):
                            act.wait_ge(route_oh, rnd * BATCHES + G * BPP + (B + 1 - G1 * BPP))
                            for i in range(RB):
                                j = G * (BPP * RB) + (B * RB + i - G1 * BPP * RB)
                                last = nc.scalar.activation(
                                    route[:, B % RING_B, i, 0:P], place[:, B % RING_B, i, :], ACT.Copy,
                                    scale=head1[:, ds(j, 1)])
                            last.then_inc(route_h, 1)
                            B += 1
                        high(rnd * GPR + G * (2 * NB) + gg, G * 2 + gg // NB, gg, gg % NB)
                G = G2
                for s in range(20):
                    if s % 2:
                        gg = s // 2
                        w_turn(rnd, G, gg)
                    if P1C[s] is not None:
                        kind, hb = A_STEPS[P1C[s]]
                        unit_step(rnd * UPR + hb, kind, hb, 0)
                    if s % 2:
                        high(rnd * GPR + G * 2 * NB + gg, G * 2 + gg // NB, gg, gg % NB)
                        if gg >= NB:
                            m = gg - NB
                            act.wait_ge(acc_ev, rnd * NB + 1)
                            nc.scalar.activation(bank[m][:, :], acc[:, m, :], ACT.Copy).then_inc(acc_in, 1)

                def relation(i, k, par, with_h):
                    for what, j in P2:
                        if what == "a":
                            kind, hb = A_STEPS[j]
                            unit_step(rnd * UPR + (i + 1) * NB + hb, kind, hb, 1 - par)
                        elif with_h:
                            gg = par * NB + j
                            w_turn(rnd, k + SLOTS // 2, gg)
                            high(rnd * GPR + k * (2 * NB) + SLOTS * NB + gg, k * 2 + par, gg, j)

                with act.Fori(0, 3) as k:
                    relation(k * 2, k, 0, True)
                    relation(k * 2 + 1, k, 1, True)
                relation(R - 2, 3, 0, False)

                act.wait_ge(xn_in, rnd * 32 + 32)
                for m in range(NB):
                    rows = P if m < NB - 1 else LASTP
                    nc.scalar.activation(xs[0:rows, m, :], xn[0:rows, m, :], ACT.Copy, scale=H_SCALE)\
                        .then_inc(xs_done, 1)
                def keep(m):
                    act.wait_ge(fin_step, fin_at(rnd, m, 1))
                    nc.scalar.activation(acc[:, m, :], bank[m][:, :], ACT.Copy).then_inc(acc_ev, 1)

                for m in range(NB):
                    rows = P if m < NB - 1 else LASTP
                    if m:
                        keep(m - 1)
                    act.wait_ge(fin_step, fin_at(rnd, m, 4))
                    nc.scalar.activation(sd[0:rows, m:m + 1], mv[0:rows, m, 1:2], ACT.Sqrt)\
                        .then_inc(sd_done, 1)
                    if m < NB - 1:
                        act.wait_ge(fin_step, fin_at(rnd, m, 6))
                        nc.scalar.activation(o[0:rows, m, :], y[0:rows, m, :], ACT.Identity,
                                             bias=shift[0:rows, m:m + 1], scale=rstd[0:rows, m:m + 1])\
                            .then_inc(o_done, 1)
                keep(NB - 1)
                act.wait_ge(b_in[0], rnd * (16 * R) + 16 * R + 16)
                act.wait_ge(rounds_done, rnd + 1)
                gate(act)
                act.reg_load(reg, rounds_i[0:1, 0:1])
                act.sem_inc(rounds_read, 1)

        @block.vector
        def _(dve):
            v = nc.vector
            dve.sem_inc(t_ev, 1)
            dve.sem_inc(rounds_read, 1)
            v.memset(zeros[:, :], 0.0).then_inc(zeros_done, 1)
            steps = [0]

            def step(ins):
                steps[0] += 1
                ins.then_inc(small, 1)
                dve.wait_ge(small, steps[0])

            def x_part(k):
                dve.wait_ge(x_hi, 2 * k + 1)
                v.scalar_tensor_tensor(XT[:, k, 1, :], x_stage[:, k, :], X_SCALE, XT[:, k, 0, :],
                                       ALU.mult, ALU.subtract).then_inc(x_lo, 1)
                dve.wait_ge(x_hi, 2 * k + 2)
                v.scalar_tensor_tensor(whl[:, 1, 1, k * D:(k + 1) * D], wf[:, 1, k * D:(k + 1) * D], W_SCALE,
                                       whl[:, 1, 0, k * D:(k + 1) * D], ALU.mult, ALU.subtract)\
                    .then_inc(x_lo, 1)

            x_part(0)
            dve.wait_ge(src_in, 16)
            dve.wait_ge(pads, 3)
            step(v.tensor_scalar(hb_f[:, :], si[:, :], float(P), None, ALU.is_ge))
            for i in range(2, NB):
                step(v.scalar_tensor_tensor(hb_f[:, :], si[:, :], float(P * i), hb_f[:, :], ALU.is_ge, ALU.add))
            dve.wait_ge(dst_in, 32)
            step(v.tensor_scalar(ts_f[:, :], di[:, :], float(TW), None, ALU.is_ge))
            step(v.scalar_tensor_tensor(ts_f[:, :], di[:, :], float(2 * TW), ts_f[:, :], ALU.is_ge, ALU.add))
            step(v.scalar_tensor_tensor(tmp_f[:, :], ei[:, :], float(NB * TS), ts_f[:, :], ALU.mult, ALU.add))
            v.scalar_tensor_tensor(key[:, :, :].rearrange("p c t -> p (c t)")[:, 0:ET], hb_f[:, :], float(TS),
                                   tmp_f[:, :], ALU.mult, ALU.add).then_inc(key_done, 1)
            for k in range(1, KD):
                x_part(k)
            step(v.tensor_scalar(head1[:, 0:ET], si[:, :], 1.0, None, ALU.add))
            step(v.scalar_tensor_tensor(head1[:, 0:ET], hb_f[:, :], -float(P), head1[:, 0:ET], ALU.mult, ALU.add))
            step(v.tensor_scalar(tail1[:, 0:ET], di[:, :], 1.0, None, ALU.add))
            step(v.scalar_tensor_tensor(tail1[:, 0:ET], ts_f[:, :], -float(TW), tail1[:, 0:ET], ALU.mult, ALU.add))

            def split_w(n, slot, k):
                dve.wait_ge(w_hi, n * KD + (k + 1))
                v.scalar_tensor_tensor(whl[:, slot, 1, k * D:(k + 1) * D], wf[:, slot, k * D:(k + 1) * D],
                                       W_SCALE, whl[:, slot, 0, k * D:(k + 1) * D],
                                       ALU.mult, ALU.subtract).then_inc(w_lo, 1)

            dve.wait_ge(x_lo, 2 * KD)
            dve.sem_inc(w_lo, KD)
            for k in range(KD):
                split_w(0, 0, k)
            dve.wait_ge(bself_in, 16)
            for m in range(NB):
                dve.wait_ge(h_mm, m + 1)
                v.scalar_tensor_tensor(acc[:, m, :], bself, H_SCALE, bank[m][:, :], ALU.mult, ALU.add)\
                    .then_inc(h_t, 1)
            dve.wait_ge(const_done, 8)
            dve.wait_ge(key_done, 1)
            reg = rounds_loop(dve)

            def evacuate(rnd, G, gg, source, shift=0):
                n = rnd * GPR + G * (2 * NB) + (gg + shift)
                if gg % NB == 0:
                    m = rnd * R + G + shift // (2 * NB)
                    dve.wait_ge(b_in[gg // NB], m * 16 + 16)
                dve.wait_ge(h_mm, n + NB + 1)
                dve.wait_ge(h_lo, n + 1)
                v.scalar_tensor_tensor(t[:, gg % 2, :], bias[:, gg // NB % 2, :], H_SCALE, source[:, :],
                                       ALU.mult, ALU.add).then_inc(h_t, 1)

            def w_turn(rnd, G, gg):
                if gg < KD:
                    split_w(rnd * SINGLES + G * 2 + 1, 1, gg)
                if NB <= gg < NB + KD:
                    split_w(rnd * SINGLES + G * 2 + 2, 0, gg - NB)

            def mask_chunk(rnd, it, c):
                dve.wait_ge(key_in[c], rnd * (16 * G1) + it * 16 + 16)
                v.tensor_scalar(kbuf[:, c, :], kbuf[:, c, :], bucket_id[0:BUCKETS, :], None, ALU.is_equal)\
                    .then_inc(mask_done, 1)

            def count_chunk(rnd, it, c):
                C = rnd * CHUNKS + it * CH_BUF + c
                dve.wait_ge(mask_done, C + 1)
                dve.wait_ge(m_done, C + 1)
                dve.wait_ge(scan_done, C + rnd + 1)
                v.tensor_tensor_scan(scan[:, c % SCANS, :], kbuf[:, c, :],
                                     zero_f[0:BUCKETS, :].to_broadcast([BUCKETS, CH_E]),
                                     scan[:, (c - 1) % SCANS, CH_E - 1:CH_E], ALU.add, ALU.add)\
                    .then_inc(scan_done, 1)

            def one_hots(U, u_local, par):
                dve.wait_ge(a_mm, U * 2 + 1)
                T = TS * HALVES
                v.tensor_tensor(ohh[:, par, :, :], iota1[:, 0:P].unsqueeze(1).to_broadcast([P, T, P]),
                                edges[:, 0, ds(u_local * T, T)].unsqueeze(2).to_broadcast([P, T, P]),
                                ALU.is_equal)
                for j in range(T):
                    c = u_local * T + j
                    last = v.tensor_scalar(oht[:, par, j, :], iota1[:, 0:TW], edges[:, 1, ds(c, 1)], None,
                                           ALU.is_equal)
                last.then_inc(a_oh, 1)

            def transposes_out(U, hb, par):
                dve.wait_ge(t_mm, U + 1)
                v.tensor_copy(AT[par][:, :, hb * P:(hb + 1) * P], b_t).then_inc(t_ev, 1)

            with dve.Fori(0, reg) as rnd:
                v.tensor_copy(scan[:, SCANS - 1, CH_E - 1:CH_E], offset[0:BUCKETS, :]).then_inc(scan_done, 1)
                with dve.Fori(0, G1) as it:
                    mask_chunk(rnd, it, 0)
                    count_chunk(rnd, it, 0)
                    for gg in range(2 * NB):
                        if gg < SEED_LEAD:
                            evacuate(rnd, it, gg, bank[gg % NB])
                        if gg + 1 < CH_BUF:
                            mask_chunk(rnd, it, gg + 1)
                        w_turn(rnd, it, gg)
                        if gg + 1 < CH_BUF:
                            count_chunk(rnd, it, gg + 1)
                        if gg >= SEED_LEAD:
                            n = rnd * GPR + it * (2 * NB) + gg
                            dve.wait_ge(h_hi, n + 1)
                            v.tensor_tensor(
                                Hb[:, ds(it * 2 + gg // NB, 1), gg % NB, 1, :].rearrange("p a d -> p (a d)"),
                                bank[gg % NB][:, :],
                                Hb[:, ds(it * 2 + gg // NB, 1), gg % NB, 0, :].rearrange("p a d -> p (a d)"),
                                ALU.subtract).then_inc(h_t, 1)

                dve.wait_ge(scan_done, rnd * (CHUNKS + 1) + CHUNKS + 1)
                v.tensor_tensor(total[0:BUCKETS, :], scan[:, SCANS - 1, CH_E - 1:CH_E], offset[0:BUCKETS, :],
                                ALU.subtract).then_inc(total_done, 1)
                dve.wait_ge(total_done, rnd + 1)
                v.tensor_scalar(offset[:, :], offset[:, :], -float(CAP), None, ALU.add).then_inc(round_step, 1)
                dve.wait_ge(rank_mm, rnd * CHUNKS + CHUNKS + CH_BUF)
                v.tensor_scalar(half[:, :], b_rank[0:EP, 0:ET_R], float(P + 1), None, ALU.is_ge)\
                    .then_inc(place_step, 1)
                dve.wait_ge(place_step, rnd * 3 + 1)
                v.scalar_tensor_tensor(lo1[:, :], half[:, :], -float(P), b_rank[0:EP, 0:ET_R], ALU.mult, ALU.add)\
                    .then_inc(place_step, 1)
                v.scalar_tensor_tensor(col[:, :], key[:, :, :].rearrange("p c t -> p (c t)")[:, 0:ET_R], float(HALVES),
                                       half[:, :], ALU.mult, ALU.add).then_inc(place_step, 1)
                dve.wait_ge(place_step, rnd * 3 + 3)
                gate(dve)

                with dve.Fori(G1, G2) as it:
                    B = 0
                    for gg in range(2 * NB):
                        for _ in range(B_MADE[gg]):
                            dve.wait_ge(route_mm, rnd * BATCHES + it * BPP + (B + 1 - G1 * BPP))
                            j = it * (BPP * RB) + (B * RB - G1 * BPP * RB)
                            v.tensor_tensor(place[:, B % RING_B, :, :],
                                            iota1[0:EP, 0:P].unsqueeze(1).to_broadcast([EP, RB, P]),
                                            lo1[:, ds(j, RB)].unsqueeze(2).to_broadcast([EP, RB, P]),
                                            ALU.is_equal)
                            for i in range(RB):
                                last = v.tensor_scalar(route[:, B % RING_B, i, 2 * P:RT_W],
                                                       iota0[0:EP, 0:COLS], col[:, ds(j + i, 1)], None,
                                                       ALU.is_equal)
                            last.then_inc(route_oh, 1)
                            B += 1
                        w_turn(rnd, it, gg)
                        evacuate(rnd, it, gg, bank[gg % NB])

                dve.wait_ge(route_mm, rnd * BATCHES + BATCHES + RING_B)
                for p in range(2):
                    v.memset(A[p][:, :, TS * TW:NP], 0.0)
                v.tensor_copy(edges[:, 0, :], b_heads[:, 0:COLS]).then_inc(sorted_done, 1)
                v.tensor_copy(edges[:, 1, :], b_tails[:, 0:COLS]).then_inc(sorted_done, 1)
                dve.wait_ge(total_mm, rnd + 1)
                v.tensor_reduce(most[:, :], b_total[0:1, :], AX.X, ALU.max).then_inc(round_step, 1)
                dve.wait_ge(sorted_done, rnd * 2 + 2)
                G = G2
                U = rnd * UPR
                one_hots(U, 0, 0)
                for s in range(20):
                    if s % 2:
                        gg = s // 2
                        evacuate(rnd, 0, gg, bank[gg % NB], G * 2 * NB)
                        w_turn(rnd, G, gg)
                    if s == 1:
                        one_hots(U + 1, 1, 1)
                    if s == 2:
                        dve.wait_ge(round_step, rnd * 4 + 2)
                        v.tensor_scalar(over[:, :], thresholds[:, :], most[0:1, 0:1], None, ALU.is_lt)\
                            .then_inc(round_step, 1)
                        dve.wait_ge(round_step, rnd * 4 + 3)
                        v.tensor_reduce(rounds_f[:, :], over[:, :], AX.X, ALU.add).then_inc(round_step, 1)
                        dve.wait_ge(round_step, rnd * 4 + 4)
                        dve.wait_ge(rounds_read, rnd * 4 + 1)
                        v.tensor_copy(rounds_i[:, :], rounds_f[:, :]).then_inc(rounds_done, 1)
                    if P1C[s] is not None:
                        kind, hb = A_STEPS[P1C[s]]
                        if kind == "T":
                            transposes_out(U + hb, hb, 0)
                        if kind == "A2":
                            one_hots(U + hb + 2, hb + 2, hb % 2)

                def relation(i, k, par, with_h):
                    u = (i + 1) * NB
                    up = (1 + par) % 2
                    for what, j in P2:
                        if what == "a":
                            kind, hb = A_STEPS[j]
                            if kind == "T":
                                transposes_out(rnd * UPR + u + hb, hb, 1 - par)
                            if kind == "A2" and (with_h or hb + 2 < NB):
                                one_hots(rnd * UPR + u + hb + 2, u + hb + 2, (up + hb) % 2)
                        elif with_h:
                            gg = par * NB + j
                            evacuate(rnd, k, gg, b_h2, SLOTS * NB)
                            w_turn(rnd, k + SLOTS // 2, gg)

                with dve.Fori(0, 3) as k:
                    relation(k * 2, k, 0, True)
                    relation(k * 2 + 1, k, 1, True)
                relation(R - 2, 3, 0, False)

                def fin(m, n):
                    dve.wait_ge(fin_step, fin_at(rnd, m, n))

                def residual(m):
                    rows = P if m < NB - 1 else LASTP
                    dve.wait_ge(xs_done, rnd * NB + m + 1)
                    dve.wait_ge(out_mm, rnd * NB + m + 1)
                    v.scalar_tensor_tensor(y[0:rows, m, :], bank[m][0:rows, :], 0.0, xs[0:rows, m, :],
                                           ALU.max, ALU.add).then_inc(fin_step, 1)

                def statistics(m):
                    rows = P if m < NB - 1 else LASTP
                    fin(m, 1)
                    v.bn_stats(stats[0:rows, m, :], y[0:rows, m, :]).then_inc(fin_step, 1)
                    fin(m, 2)
                    gate(dve)
                    v.bn_aggr(mv[0:rows, m, :], stats[0:rows, m, :]).then_inc(fin_step, 1)
                    fin(m, 3)
                    v.tensor_scalar(mv[0:rows, m, 1:2], mv[0:rows, m, 1:2], EPS * H_SCALE ** 2, None, ALU.add)\
                        .then_inc(fin_step, 1)

                def normalise(m):
                    rows = P if m < NB - 1 else LASTP
                    dve.wait_ge(sd_first, 1)
                    dve.wait_ge(sd_done, rnd * NB + m + 1)
                    v.reciprocal(rstd[0:rows, m:m + 1], sd[0:rows, m:m + 1]).then_inc(fin_step, 1)
                    fin(m, 5)
                    if m < NB - 1:
                        v.scalar_tensor_tensor(shift[0:rows, m:m + 1], mv[0:rows, m, 0:1], -1.0,
                                               rstd[0:rows, m:m + 1], ALU.mult, ALU.mult).then_inc(fin_step, 1)
                    else:
                        v.tensor_scalar(o[0:rows, m, :], y[0:rows, m, :], mv[0:rows, m, 0:1],
                                        rstd[0:rows, m:m + 1], ALU.subtract, ALU.mult).then_inc(o_done, 1)

                for m in range(NB):
                    residual(m)
                    statistics(m)
                    normalise(m)
                dve.reg_load(reg, rounds_i[0:1, 0:1])
                dve.wait_ge(o_done, rnd * NB + NB)
                dve.wait_ge(round_step, rnd * 4 + 4)

        @block.tensor
        def _(pe):
            pe.sem_inc(rank_mm, CH_BUF)
            pe.sem_inc(route_mm, RING_B)
            pe.sem_inc(a_mm, 3)

            def h_products(dest, m, wslot, part=None, seeded=False):
                mm = []
                for k in range(KD):
                    for xh, wh in ((0, 0), (0, 1), (1, 0)):
                        mm.append((k, xh, wh))
                todo = mm if part is None else mm[part * 6:part * 6 + 6]
                for k, xh, wh in todo:
                    last = nc.tensor.matmul(dest[:, :], XT[:, k, xh, m * P:(m + 1) * P],
                                            whl[:, wslot, wh, k * D:(k + 1) * D],
                                            start=(k, xh, wh) == mm[0] and not seeded,
                                            stop=(k, xh, wh) == mm[-1], skip_group_check=seeded)
                if part != 0:
                    last.then_inc(h_mm, 1)

            pe.wait_ge(zeros_done, 1)
            for _ in range(WARM_UP):
                nc.tensor.matmul(b_rank[:, 0:P], zeros[:, :], zeros[:, :], start=True, stop=True)

            for k in range(KD - 1):
                for xh, wh in ((0, 0), (1, 0), (0, 1)):
                    pe.wait_ge(x_hi, 2 * k + 2)
                    pe.wait_ge(x_lo, 2 * k + xh + 2 * wh)
                    for m in range(NB):
                        nc.tensor.matmul(bank[m][:, :], XT[:, k, xh, m * P:(m + 1) * P],
                                         whl[:, 1, wh, k * D:(k + 1) * D], start=(k, xh, wh) == (0, 0, 0),
                                         stop=False)
            k = KD - 1
            pe.wait_ge(x_lo, 2 * KD)
            for m in range(NB):
                for xh, wh in ((0, 0), (0, 1), (1, 0)):
                    last = nc.tensor.matmul(bank[m][:, :], XT[:, k, xh, m * P:(m + 1) * P],
                                            whl[:, 1, wh, k * D:(k + 1) * D], start=False,
                                            stop=(xh, wh) == (1, 0))
                last.then_inc(h_mm, 1)
            pe.wait_ge(const_done, 8)
            reg = rounds_loop(pe)

            def group(n, S, gg, part=None, seed=None):
                if part != 1:
                    if gg % NB == 0:
                        pe.wait_ge(w_lo, S * KD + 2 * KD)
                    if seed is None:
                        pe.wait_ge(h_t, n + 1)
                    else:
                        pe.wait_ge(h_seed, seed)
                h_products(bank[gg % NB], gg % NB, gg // NB, part, seed is not None)

            def unit_step(U, kind, hb, par, up):
                if kind == "A01":
                    pe.wait_ge(a_oh, U + 1)
                    pe.wait_ge(a_ev, U * 2 + 1)
                    for j in range(2 * HALVES):
                        ts = j // HALVES
                        last = nc.tensor.matmul(b_a[:, ts * TW:(ts + 1) * TW], ohh[:, up, j, :], oht[:, up, j, :],
                                                start=j % HALVES == 0, stop=j % HALVES == HALVES - 1)
                    last.then_inc(a_mm, 1)
                if kind == "A2":
                    pe.wait_ge(a_ev, U * 2 + 2)
                    for j in range(2 * HALVES, 3 * HALVES):
                        last = nc.tensor.matmul(b_a[:, 0:TW], ohh[:, up, j, :], oht[:, up, j, :],
                                                start=j % HALVES == 0, stop=j % HALVES == HALVES - 1)
                    last.then_inc(a_mm, 1)
                if kind == "T":
                    pe.wait_ge(a_ev, U * 2 + 3)
                    pe.wait_ge(t_ev, U + 1)
                    for tb in range(NB):
                        last = nc.tensor.transpose(b_t[:, tb, :], A[par][:, hb, tb * P:(tb + 1) * P], ident[:, :])
                    last.then_inc(t_mm, 1)

            with pe.Fori(0, reg) as rnd:
                pe.wait_ge(acc_ev, rnd * NB + 1)
                gate(pe)
                with pe.Fori(0, G1) as it:
                    for gg in range(2 * NB):
                        group(rnd * GPR + it * (2 * NB) + gg, rnd * SINGLES + it * 2 + gg // NB, gg,
                              seed=None if gg < SEED_LEAD
                              else rnd * (G1 * SEEDS) + it * SEEDS + (gg - SEED_LEAD + 1))
                        c = gg - CH_LAG
                        if c < 0:
                            continue
                        pe.wait_ge(m_done, rnd * CHUNKS + it * CH_BUF + (c + 1 + SCANS))
                        tiles = kbuf[:, c, :].rearrange("b (p t) -> b t p", t=CH_T)
                        for i in range(CH_T):
                            last = nc.tensor.matmul(b_rank[0:EP, ds(it * (CH_BUF * CH_T) + c * CH_T + i, 1)],
                                                    tiles[:, i, :], ones[0:BUCKETS, 0:1],
                                                    start=True, stop=True)
                        last.then_inc(rank_mm, 1)
                for dest in (b_heads, b_tails):
                    nc.tensor.matmul(dest[:, 0:COLS], zeros[:, :], whl[:, 0, 0, 0:COLS], start=True, stop=False,
                                     skip_group_check=True)


                with pe.Fori(G1, G2) as it:
                    B = 0
                    for gg in range(2 * NB):
                        group(rnd * GPR + it * (2 * NB) + gg, rnd * SINGLES + it * 2 + gg // NB, gg)
                        for _ in range(B_USED[gg]):
                            n = rnd * BATCHES + it * BPP + (B + 1 - G1 * BPP)
                            pe.wait_ge(route_h, n)
                            pe.wait_ge(route_t, n)
                            for i in range(RB):
                                o_h = route[:, B % RING_B, i, :]
                                nc.tensor.matmul(b_heads[:, 0:COLS], o_h[:, 0:P], o_h[:, 2 * P:RT_W],
                                                 start=False, stop=False, skip_group_check=True)
                                last = nc.tensor.matmul(b_tails[:, 0:COLS], o_h[:, P:2 * P], o_h[:, 2 * P:RT_W],
                                                        start=False, stop=False, skip_group_check=True)
                            last.then_inc(route_mm, 1)
                            B += 1

                pe.wait_ge(place_step, rnd * 3 + 2)
                pe.wait_ge(total_done, rnd + 1)
                nc.tensor.matmul(b_total[0:1, :], total[0:BUCKETS, :], ident_f[0:BUCKETS, 0:BUCKETS],
                                 start=True, stop=True).then_inc(total_mm, 1)

                G = G2
                for s in range(20):
                    if s == min(s for s in range(20) if P1C[s] is not None):
                        pe.wait_ge(round_step, rnd * 4 + 2)
                    gg = s // 2
                    group(rnd * GPR + G * 2 * NB + gg, rnd * SINGLES + G * 2 + gg // NB, gg, s % 2)
                    if P1C[s] is not None:
                        kind, hb = A_STEPS[P1C[s]]
                        unit_step(rnd * UPR + hb, kind, hb, 0, hb % 2)

                def relation(i, k, slot, par, build_next, with_h):
                    up = (1 + par) % 2
                    pe.wait_ge(h_lo, rnd * GPR + (i * 2 + 1) * NB + 2)
                    for s, (what, j) in enumerate(P2):
                        if s == 10:
                            pe.wait_ge(h_lo, rnd * GPR + (i * 2 + 2) * NB + 2)
                        d, nb = s // 10, s % 10 // 2
                        lhs = (AT, A)[d][par]
                        if d == 0 and s % 2 == 0:
                            if par == 0 and with_h:
                                pe.wait_ge(acc_in, rnd * NB + nb + 1)
                            pe.wait_ge(t_ev, rnd * UPR + i * NB + (nb + 2))
                        for kb in ((0, 1, 2), (3, 4))[s % 2]:
                            for hl in range(2):
                                last = nc.tensor.matmul(
                                    bank[nb][:, :], lhs[:, kb, nb * P:(nb + 1) * P],
                                    Hb[:, ds(slot + d, 1), kb, hl, :].rearrange("p a d -> p (a d)"),
                                    start=False, stop=not build_next and s == 10 + nb * 2 + 1,
                                    skip_group_check=True)
                        if not build_next and s >= 10 and s % 2:
                            last.then_inc(out_mm, 1)
                        if what == "a" and build_next:
                            kind, hb = A_STEPS[j]
                            unit_step(rnd * UPR + (i + 1) * NB + hb, kind, hb, 1 - par, (up + hb) % 2)
                        if what == "h" and with_h:
                            if j == 0:
                                pe.wait_ge(w_lo, rnd * (SINGLES * KD) + k * (2 * KD) + (SLOTS + par + 2) * KD)
                            pe.wait_ge(h_t, rnd * GPR + k * (2 * NB) + (SLOTS * NB + par * NB + j + NB))
                            h_products(b_h2, j, par)

                with pe.Fori(0, 3) as k:
                    relation(k * 2, k, k * 4, 0, True, True)
                    relation(k * 2 + 1, k, (k * 4 + 2) % SLOTS, 1, True, True)
                relation(R - 2, 3, 2, 0, True, False)
                relation(R - 1, 3, 4, 1, False, False)
                pe.wait_ge(rounds_done, rnd + 1)
                gate(pe)
                pe.reg_load(reg, rounds_i[0:1, 0:1])
                pe.sem_inc(rounds_read, 1)


def kernel(**inputs):
    import numpy as np
    import concourse.bacc as bacc
    from concourse import mybir
    from concourse.bass_utils import run_bass_kernel_spmd

    def tiles(a):
        return np.ascontiguousarray(np.asarray(a).reshape(EP, ET))

    def weights(a):
        a = np.asarray(a)
        a = np.swapaxes(a, -1, -2).reshape(*a.shape[:-2], KD, P, D)
        return np.ascontiguousarray(np.swapaxes(a, -2, -3).reshape(*a.shape[:-3], P, KD * D))

    order = [d * R + r for r in range(R) for d in range(2)]
    x = np.ascontiguousarray(inputs["x"])
    xt = np.zeros((KD, P, NP), x.dtype)
    xt[:, :, :N] = x.T.reshape(KD, P, N)
    arrays = {
        "x": x,
        "xt": np.ascontiguousarray(xt.transpose(1, 0, 2)),
        "src": tiles(inputs["src"]),
        "dst": tiles(inputs["dst"]),
        "et": tiles(inputs["edge_type_8"]),
        "w_self": weights(inputs["L0_gnn_W_self"]),
        "b_self": np.asarray(inputs["L0_gnn_b_self"]).reshape(1, D),
        "w": weights(inputs["L0_gnn_W_rel"])[order],
        "b": np.asarray(inputs["L0_gnn_b_rel"])[order],
    }
    arrays = {f"in_{k}_dram": np.ascontiguousarray(v) for k, v in arrays.items()}
    nc = bacc.Bacc("TRN2", target_bir_lowering=False, num_devices=1)
    args = [nc.dram_tensor(k, v.shape, mybir.dt.from_np(v.dtype), kind="ExternalInput").ap()
            for k, v in arrays.items()]
    out = nc.dram_tensor("out_dram", (N, D), mybir.dt.float32, kind="ExternalOutput").ap()
    build(nc, *args, out)
    result = run_bass_kernel_spmd(nc, [arrays], core_ids=[0])
    return result.results[0]["out_dram"]
```
